# Optimizing a Trainium2 kernel written in Bass

```python
import numpy as np
import jax
import jax.numpy as jnp

def _softmax(x, axis=-1):
    return jax.nn.softmax(x, axis=axis)

def _gelu(x):
    return jax.nn.gelu(x, approximate=True)

def _silu(x):
    return jax.nn.silu(x)

def _sigmoid(x):
    return jax.nn.sigmoid(x)

def _layernorm(x, axis=-1, eps=1e-05):
    m = jnp.mean(x, axis=axis, keepdims=True)
    v = jnp.var(x, axis=axis, keepdims=True)
    return (x - m) / jnp.sqrt(v + eps)

def _scatter_add(tgt, idx, src, axis=0):
    return tgt.at[idx].add(src)

def _segment_sum(src, seg, n):
    return jax.ops.segment_sum(src, seg, n)
kernel_name = 'mk_gnn_resnorm_d4_gnn_r8_fd7cbe'

def setup_inputs(seed: int=0):
    np.random.seed(seed)
    _w = jnp.asarray

    def _rec_inputs():
        import jax
        import jax.numpy as jnp
        _gk = jax.random.key(seed)
        x = -0.0005121 + 1.001 * jax.random.normal(jax.random.fold_in(_gk, 1), (12500, 32), jnp.float32)
        src = jax.random.randint(jax.random.fold_in(_gk, 2), (400000,), 0, 12500, jnp.int32)
        dst = jnp.minimum((12500 * jax.random.uniform(jax.random.fold_in(_gk, 3), (400000,)) ** 2.0).astype(jnp.int32), 99999)
        _o = jnp.argsort(dst, stable=True)
        src = src[_o]
        dst = dst[_o]
        edge_attr_16 = 0.000196303 + 1.00016 * jax.random.normal(jax.random.fold_in(_gk, 12), (400000, 16), jnp.float32)
        edge_attr_3 = 0.000549083 + 1.00031 * jax.random.normal(jax.random.fold_in(_gk, 13), (400000, 3), jnp.float32)
        edge_attr_32 = 0.000216709 + 1.00012 * jax.random.normal(jax.random.fold_in(_gk, 14), (400000, 32), jnp.float32)
        edge_attr_4 = 0.000714719 + 1.00021 * jax.random.normal(jax.random.fold_in(_gk, 15), (400000, 4), jnp.float32)
        edge_attr_5 = -0.000325185 + 1.00005 * jax.random.normal(jax.random.fold_in(_gk, 16), (400000, 5), jnp.float32)
        edge_weight1 = 0.000452788 + 0.999756 * jax.random.normal(jax.random.fold_in(_gk, 18), (400000, 1), jnp.float32)
        return (x, src, dst, edge_attr_16, edge_attr_3, edge_attr_32, edge_attr_4, edge_attr_5, edge_weight1)
    x, src, dst, edge_attr_16, edge_attr_3, edge_attr_32, edge_attr_4, edge_attr_5, edge_weight1 = _rec_inputs()

    def _L0_gnn_setup():
        import jax, jax.numpy as jnp
        import numpy as np
        MUL = 8
        N_NODES = 12500
        N_EDGES = 100000
        EDGE_DIM = 32
        MLP_DIM = 64
        W_NUMEL = 4 * MUL * MUL
        ALPHA = 0.25
        C110 = 1.0 / np.sqrt(3.0)
        SI_SCALE = 1.0 / np.sqrt(MUL)
        key = jax.random.key(seed)
        ks = jax.random.split(key, 10)
        node_attr = jax.random.normal(ks[0], (N_NODES, 4 * MUL), dtype=jnp.float32)
        edge_index = jax.random.randint(ks[1], (2, N_EDGES), 0, N_NODES, dtype=jnp.int64)
        edge_sh = jax.random.normal(ks[2], (N_EDGES, 4), dtype=jnp.float32)
        edge_feat = jax.random.normal(ks[3], (N_EDGES, EDGE_DIM), dtype=jnp.float32)
        W1 = jax.random.normal(ks[4], (EDGE_DIM, MLP_DIM), dtype=jnp.float32) / np.sqrt(EDGE_DIM)
        b1 = jnp.zeros((MLP_DIM,), dtype=jnp.float32)
        W2 = jax.random.normal(ks[5], (MLP_DIM, W_NUMEL), dtype=jnp.float32) / np.sqrt(MLP_DIM)
        b2 = jnp.zeros((W_NUMEL,), dtype=jnp.float32)
        si_w0 = jax.random.normal(ks[6], (MUL, MUL), dtype=jnp.float32)
        si_w1 = jax.random.normal(ks[7], (MUL, MUL), dtype=jnp.float32)
        return {'node_attr': node_attr, 'edge_index': edge_index, 'edge_sh': edge_sh, 'edge_feat': edge_feat, 'W1': W1, 'b1': b1, 'W2': W2, 'b2': b2, 'si_w0': si_w0, 'si_w1': si_w1}
    _L0_gnn_all = _L0_gnn_setup()
    _L0_gnn_in = {k: v for k, v in _L0_gnn_all.items() if k in ('W1', 'b1', 'W2', 'b2', 'si_w0', 'si_w1')}
    del _L0_gnn_all

    def _L1_gnn_setup():
        import jax, jax.numpy as jnp
        import numpy as np
        import math
        M = 8
        COMBOS = [(0, 0, 0), (0, 1, 1), (1, 0, 1), (1, 1, 0), (1, 1, 1), (2, 1, 1)]

        def _cg_coeff(j1, m1, j2, m2, j3, m3):
            if m3 != m1 + m2:
                return 0.0
            f = math.factorial
            vmin = max(0, j2 - j3 - m1, j1 + m2 - j3)
            vmax = min(j1 + j2 - j3, j1 - m1, j2 + m2)
            pref = (2 * j3 + 1) * f(j3 + j1 - j2) * f(j3 - j1 + j2) * f(j1 + j2 - j3) / f(j1 + j2 + j3 + 1)
            pref *= f(j3 + m3) * f(j3 - m3) * f(j1 - m1) * f(j1 + m1) * f(j2 - m2) * f(j2 + m2)
            s = 0.0
            for v in range(vmin, vmax + 1):
                s += (-1) ** v / (f(v) * f(j1 + j2 - j3 - v) * f(j1 - m1 - v) * f(j2 + m2 - v) * f(j3 - j2 + m1 + v) * f(j3 - j1 - m2 + v))
            return math.sqrt(pref) * s

        def _su2_cg(l1, l2, l3):
            C = np.zeros((2 * l1 + 1, 2 * l2 + 1, 2 * l3 + 1), dtype=np.complex128)
            for m1 in range(-l1, l1 + 1):
                for m2 in range(-l2, l2 + 1):
                    m3 = m1 + m2
                    if -l3 <= m3 <= l3:
                        C[m1 + l1, m2 + l2, m3 + l3] = _cg_coeff(l1, m1, l2, m2, l3, m3)
            return C

        def _qmat(l):
            q = np.zeros((2 * l + 1, 2 * l + 1), dtype=np.complex128)
            for m in range(-l, 0):
                q[l + m, l + abs(m)] = 1 / np.sqrt(2)
                q[l + m, l - abs(m)] = -1j / np.sqrt(2)
            q[l, l] = 1.0
            for m in range(1, l + 1):
                q[l + m, l + abs(m)] = (-1) ** m / np.sqrt(2)
                q[l + m, l - abs(m)] = 1j * (-1) ** m / np.sqrt(2)
            return (-1j) ** l * q

        def _so3_cg(l1, l2, l3):
            C = np.einsum('ij,kl,mn,ikn->jlm', _qmat(l1), _qmat(l2), np.conj(_qmat(l3)).T, _su2_cg(l1, l2, l3))
            assert np.abs(C.imag).max() < 1e-06
            C = C.real
            return C / np.linalg.norm(C)
        CG = {c: jnp.asarray(_so3_cg(*c), dtype=jnp.float32) for c in COMBOS}
        N, E = (12500, 200000)
        ks = jax.random.split(jax.random.key(seed), 6)
        return {'node_irreps': jax.random.normal(ks[0], (N, 4 * M), jnp.float32), 'edge_index': jax.random.randint(ks[1], (2, E), 0, N, dtype=jnp.int32), 'sh0': jax.random.normal(ks[2], (E, 1), jnp.float32), 'sh1': jax.random.normal(ks[3], (E, 3), jnp.float32), 'sh2': jax.random.normal(ks[4], (E, 5), jnp.float32), 'W': jax.random.normal(ks[5], (len(COMBOS), M, M), jnp.float32)}
    _L1_gnn_all = _L1_gnn_setup()
    _L1_gnn_in = {k: v for k, v in _L1_gnn_all.items() if k in ('W',)}
    del _L1_gnn_all

    def _L2_gnn_setup():
        import jax, jax.numpy as jnp
        import numpy as np
        N_NODES = 12500
        N_EDGES = 200000
        IN_FEAT = 32
        OUT_FEAT = 32

        def _gna_forward(feat, src, dst, w1_W, w1_b, w2_W, w2_b, a):
            n = feat.shape[0]
            h_src = feat[src]
            h_dst = feat[dst]
            dt = h_dst - h_src
            a_vec = a[0]
            aij = dt @ (w2_W.T @ a_vec) + jnp.dot(a_vec, w2_b)
            ss = h_src @ w2_W.T + w2_b
            m = jax.ops.segment_max(aij, dst, num_segments=n)
            aexp = jnp.exp(aij - m[dst])
            denom = jax.ops.segment_sum(aexp, dst, num_segments=n)
            alpha = aexp / denom[dst]
            res = jax.ops.segment_sum(alpha[:, None] * ss, dst, num_segments=n)
            out = res + feat @ w1_W.T + w1_b
            return out
        key = jax.random.key(seed)
        k = jax.random.split(key, 8)
        feat = jax.random.normal(k[0], (N_NODES, IN_FEAT), dtype=jnp.float32)
        src = jax.random.randint(k[1], (N_EDGES,), 0, N_NODES, dtype=jnp.int64)
        dst = jax.random.randint(k[2], (N_EDGES,), 0, N_NODES, dtype=jnp.int64)
        s1 = 1.0 / np.sqrt(IN_FEAT)
        w1_W = jax.random.uniform(k[3], (OUT_FEAT, IN_FEAT), jnp.float32, -s1, s1)
        w1_b = jax.random.uniform(k[4], (OUT_FEAT,), jnp.float32, -s1, s1)
        w2_W = jax.random.uniform(k[5], (OUT_FEAT, IN_FEAT), jnp.float32, -s1, s1)
        w2_b = jax.random.uniform(k[6], (OUT_FEAT,), jnp.float32, -s1, s1)
        a = jax.random.normal(k[7], (1, OUT_FEAT), dtype=jnp.float32)
        return {'feat': feat, 'src': src, 'dst': dst, 'w1_W': w1_W, 'w1_b': w1_b, 'w2_W': w2_W, 'w2_b': w2_b, 'a': a}
    _L2_gnn_all = _L2_gnn_setup()
    _L2_gnn_in = {k: v for k, v in _L2_gnn_all.items() if k in ('w1_W', 'w1_b', 'w2_W', 'w2_b', 'a')}
    del _L2_gnn_all

    def _L3_gnn_setup():
        import jax, jax.numpy as jnp
        import numpy as np
        N_NODES = 6250
        N_EDGES = 200000
        D_NODE = 32
        D_EDGE = 16
        H = 64
        F_OUT = 32
        N_OUT = 32

        def _mlp_params(key, d_in, d_h, d_out):
            k1, k2 = jax.random.split(key)
            s1 = 1.0 / np.sqrt(d_in)
            s2 = 1.0 / np.sqrt(d_h)
            return (jax.random.uniform(k1, (d_in, d_h), jnp.float32, -s1, s1), jnp.zeros((d_h,), jnp.float32), jax.random.uniform(k2, (d_h, d_out), jnp.float32, -s2, s2), jnp.zeros((d_out,), jnp.float32))

        def _mlp(h, W1, b1, W2, b2):
            return jax.nn.relu(jax.nn.relu(h @ W1 + b1) @ W2 + b2)
        key = jax.random.key(seed)
        kx, ke, ka, kf, kb, kn = jax.random.split(key, 6)
        x = jax.random.normal(kx, (N_NODES, D_NODE), jnp.float32)
        edge_index = jax.random.randint(ke, (2, N_EDGES), 0, N_NODES, jnp.int64)
        edge_attr = jax.random.normal(ka, (N_EDGES, D_EDGE), jnp.float32)
        d_flow_in = 2 * D_NODE + D_EDGE
        W1f, b1f, W2f, b2f = _mlp_params(kf, d_flow_in, H, F_OUT)
        W1b, b1b, W2b, b2b = _mlp_params(kb, d_flow_in, H, F_OUT)
        W1n, b1n, W2n, b2n = _mlp_params(kn, 2 * F_OUT, H, N_OUT)
        return dict(x=x, edge_index=edge_index, edge_attr=edge_attr, W1f=W1f, b1f=b1f, W2f=W2f, b2f=b2f, W1b=W1b, b1b=b1b, W2b=W2b, b2b=b2b, W1n=W1n, b1n=b1n, W2n=W2n, b2n=b2n)
    _L3_gnn_all = _L3_gnn_setup()
    _L3_gnn_in = {k: v for k, v in _L3_gnn_all.items() if k in ('W1f', 'b1f', 'W2f', 'b2f', 'W1b', 'b1b', 'W2b', 'b2b', 'W1n', 'b1n', 'W2n', 'b2n')}
    del _L3_gnn_all
    return {'x': x, 'src': src, 'dst': dst, 'edge_attr_16': edge_attr_16, 'edge_attr_3': edge_attr_3, 'edge_attr_32': edge_attr_32, 'edge_attr_4': edge_attr_4, 'edge_attr_5': edge_attr_5, 'edge_weight1': edge_weight1, 'L0_gnn_W1': _L0_gnn_in['W1'], 'L0_gnn_b1': _L0_gnn_in['b1'], 'L0_gnn_W2': _L0_gnn_in['W2'], 'L0_gnn_b2': _L0_gnn_in['b2'], 'L0_gnn_si_w0': _L0_gnn_in['si_w0'], 'L0_gnn_si_w1': _L0_gnn_in['si_w1'], 'L1_gnn_W': _L1_gnn_in['W'], 'L2_gnn_w1_W': _L2_gnn_in['w1_W'], 'L2_gnn_w1_b': _L2_gnn_in['w1_b'], 'L2_gnn_w2_W': _L2_gnn_in['w2_W'], 'L2_gnn_w2_b': _L2_gnn_in['w2_b'], 'L2_gnn_a': _L2_gnn_in['a'], 'L3_gnn_W1f': _L3_gnn_in['W1f'], 'L3_gnn_b1f': _L3_gnn_in['b1f'], 'L3_gnn_W2f': _L3_gnn_in['W2f'], 'L3_gnn_b2f': _L3_gnn_in['b2f'], 'L3_gnn_W1b': _L3_gnn_in['W1b'], 'L3_gnn_b1b': _L3_gnn_in['b1b'], 'L3_gnn_W2b': _L3_gnn_in['W2b'], 'L3_gnn_b2b': _L3_gnn_in['b2b'], 'L3_gnn_W1n': _L3_gnn_in['W1n'], 'L3_gnn_b1n': _L3_gnn_in['b1n'], 'L3_gnn_W2n': _L3_gnn_in['W2n'], 'L3_gnn_b2n': _L3_gnn_in['b2n']}

def reference(x, src, dst, edge_attr_16, edge_attr_3, edge_attr_32, edge_attr_4, edge_attr_5, edge_weight1, L0_gnn_W1, L0_gnn_b1, L0_gnn_W2, L0_gnn_b2, L0_gnn_si_w0, L0_gnn_si_w1, L1_gnn_W, L2_gnn_w1_W, L2_gnn_w1_b, L2_gnn_w2_W, L2_gnn_w2_b, L2_gnn_a, L3_gnn_W1f, L3_gnn_b1f, L3_gnn_W2f, L3_gnn_b2f, L3_gnn_W1b, L3_gnn_b1b, L3_gnn_W2b, L3_gnn_b2b, L3_gnn_W1n, L3_gnn_b1n, L3_gnn_W2n, L3_gnn_b2n):
    import jax
    import jax.numpy as jnp

    def _L0_gnn_ref(node_attr, edge_index, edge_sh, edge_feat, W1, b1, W2, b2, si_w0, si_w1):
        import jax, jax.numpy as jnp
        import numpy as np
        MUL = 8
        N_NODES = 12500
        N_EDGES = 100000
        EDGE_DIM = 32
        MLP_DIM = 64
        W_NUMEL = 4 * MUL * MUL
        ALPHA = 0.25
        C110 = 1.0 / np.sqrt(3.0)
        SI_SCALE = 1.0 / np.sqrt(MUL)
        n = node_attr.shape[0]
        e = edge_sh.shape[0]
        h = jax.nn.relu(edge_feat @ W1 + b1)
        w = (h @ W2 + b2).reshape(e, 4, MUL, MUL)
        w_000, w_011, w_101, w_110 = (w[:, 0], w[:, 1], w[:, 2], w[:, 3])
        s = node_attr[:, :MUL]
        v = node_attr[:, MUL:].reshape(n, MUL, 3)
        src, dst = (edge_index[0], edge_index[1])
        s_e = s[src]
        v_e = v[src]
        sh0 = edge_sh[:, 0]
        sh1 = edge_sh[:, 1:4]
        m0 = ALPHA * (jnp.einsum('ei,eio->eo', s_e * sh0[:, None], w_000) + C110 * jnp.einsum('eim,em,eio->eo', v_e, sh1, w_110))
        m1 = ALPHA * (jnp.einsum('ei,em,eio->eom', s_e, sh1, w_011) + jnp.einsum('eim,eio->eom', v_e * sh0[:, None, None], w_101))
        out0 = jax.ops.segment_sum(m0, dst, num_segments=n)
        out1 = jax.ops.segment_sum(m1.reshape(e, MUL * 3), dst, num_segments=n).reshape(n, MUL, 3)
        out0 = out0 + SI_SCALE * (s @ si_w0)
        out1 = out1 + SI_SCALE * jnp.einsum('nim,io->nom', v, si_w1)
        return jnp.concatenate([out0, out1.reshape(n, MUL * 3)], axis=-1)

    def _L1_gnn_ref(node_irreps, edge_index, sh0, sh1, sh2, W):
        import jax, jax.numpy as jnp
        import numpy as np
        import math
        M = 8
        COMBOS = [(0, 0, 0), (0, 1, 1), (1, 0, 1), (1, 1, 0), (1, 1, 1), (2, 1, 1)]

        def _cg_coeff(j1, m1, j2, m2, j3, m3):
            if m3 != m1 + m2:
                return 0.0
            f = math.factorial
            vmin = max(0, j2 - j3 - m1, j1 + m2 - j3)
            vmax = min(j1 + j2 - j3, j1 - m1, j2 + m2)
            pref = (2 * j3 + 1) * f(j3 + j1 - j2) * f(j3 - j1 + j2) * f(j1 + j2 - j3) / f(j1 + j2 + j3 + 1)
            pref *= f(j3 + m3) * f(j3 - m3) * f(j1 - m1) * f(j1 + m1) * f(j2 - m2) * f(j2 + m2)
            s = 0.0
            for v in range(vmin, vmax + 1):
                s += (-1) ** v / (f(v) * f(j1 + j2 - j3 - v) * f(j1 - m1 - v) * f(j2 + m2 - v) * f(j3 - j2 + m1 + v) * f(j3 - j1 - m2 + v))
            return math.sqrt(pref) * s

        def _su2_cg(l1, l2, l3):
            C = np.zeros((2 * l1 + 1, 2 * l2 + 1, 2 * l3 + 1), dtype=np.complex128)
            for m1 in range(-l1, l1 + 1):
                for m2 in range(-l2, l2 + 1):
                    m3 = m1 + m2
                    if -l3 <= m3 <= l3:
                        C[m1 + l1, m2 + l2, m3 + l3] = _cg_coeff(l1, m1, l2, m2, l3, m3)
            return C

        def _qmat(l):
            q = np.zeros((2 * l + 1, 2 * l + 1), dtype=np.complex128)
            for m in range(-l, 0):
                q[l + m, l + abs(m)] = 1 / np.sqrt(2)
                q[l + m, l - abs(m)] = -1j / np.sqrt(2)
            q[l, l] = 1.0
            for m in range(1, l + 1):
                q[l + m, l + abs(m)] = (-1) ** m / np.sqrt(2)
                q[l + m, l - abs(m)] = 1j * (-1) ** m / np.sqrt(2)
            return (-1j) ** l * q

        def _so3_cg(l1, l2, l3):
            C = np.einsum('ij,kl,mn,ikn->jlm', _qmat(l1), _qmat(l2), np.conj(_qmat(l3)).T, _su2_cg(l1, l2, l3))
            assert np.abs(C.imag).max() < 1e-06
            C = C.real
            return C / np.linalg.norm(C)
        CG = {c: jnp.asarray(_so3_cg(*c), dtype=jnp.float32) for c in COMBOS}
        N, E = (node_irreps.shape[0], edge_index.shape[1])
        src = node_irreps[edge_index[0]]
        feats = {0: src[:, :M][:, :, None], 1: src[:, M:].reshape(E, M, 3)}
        sh = {0: sh0, 1: sh1, 2: sh2}
        msg = {0: jnp.zeros((E, M, 1), node_irreps.dtype), 1: jnp.zeros((E, M, 3), node_irreps.dtype)}
        for idx, (le, ln, lo) in enumerate(COMBOS):
            base = jnp.einsum('ijk,ei,emj->emk', CG[le, ln, lo], sh[le], feats[ln])
            msg[lo] = msg[lo] + jnp.einsum('io,eik->eok', W[idx], base)
        tgt = edge_index[1]
        agg0 = jax.ops.segment_sum(msg[0].reshape(E, M), tgt, num_segments=N)
        agg1 = jax.ops.segment_sum(msg[1].reshape(E, 3 * M), tgt, num_segments=N)
        return jnp.concatenate([agg0, agg1], axis=1)

    def _L2_gnn_ref(feat, src, dst, w1_W, w1_b, w2_W, w2_b, a):
        import jax, jax.numpy as jnp
        import numpy as np
        N_NODES = 12500
        N_EDGES = 200000
        IN_FEAT = 32
        OUT_FEAT = 32

        def _gna_forward(feat, src, dst, w1_W, w1_b, w2_W, w2_b, a):
            n = feat.shape[0]
            h_src = feat[src]
            h_dst = feat[dst]
            dt = h_dst - h_src
            a_vec = a[0]
            aij = dt @ (w2_W.T @ a_vec) + jnp.dot(a_vec, w2_b)
            ss = h_src @ w2_W.T + w2_b
            m = jax.ops.segment_max(aij, dst, num_segments=n)
            aexp = jnp.exp(aij - m[dst])
            denom = jax.ops.segment_sum(aexp, dst, num_segments=n)
            alpha = aexp / denom[dst]
            res = jax.ops.segment_sum(alpha[:, None] * ss, dst, num_segments=n)
            out = res + feat @ w1_W.T + w1_b
            return out
        return _gna_forward(feat, src, dst, w1_W, w1_b, w2_W, w2_b, a)

    def _L3_gnn_ref(x, edge_index, edge_attr, W1f, b1f, W2f, b2f, W1b, b1b, W2b, b2b, W1n, b1n, W2n, b2n):
        import jax, jax.numpy as jnp
        import numpy as np
        N_NODES = 6250
        N_EDGES = 200000
        D_NODE = 32
        D_EDGE = 16
        H = 64
        F_OUT = 32
        N_OUT = 32

        def _mlp_params(key, d_in, d_h, d_out):
            k1, k2 = jax.random.split(key)
            s1 = 1.0 / np.sqrt(d_in)
            s2 = 1.0 / np.sqrt(d_h)
            return (jax.random.uniform(k1, (d_in, d_h), jnp.float32, -s1, s1), jnp.zeros((d_h,), jnp.float32), jax.random.uniform(k2, (d_h, d_out), jnp.float32, -s2, s2), jnp.zeros((d_out,), jnp.float32))

        def _mlp(h, W1, b1, W2, b2):
            return jax.nn.relu(jax.nn.relu(h @ W1 + b1) @ W2 + b2)
        past, future = (edge_index[0], edge_index[1])
        x_past = x[past]
        x_future = x[future]
        fwd_in = jnp.concatenate([x_future, x_past, edge_attr], axis=1)
        flow_fwd = _mlp(fwd_in, W1f, b1f, W2f, b2f)
        fwd_agg = jax.ops.segment_sum(flow_fwd, future, num_segments=x.shape[0])
        bwd_in = jnp.concatenate([x_past, x_future, edge_attr], axis=1)
        flow_bwd = _mlp(bwd_in, W1b, b1b, W2b, b2b)
        bwd_agg = jax.ops.segment_sum(flow_bwd, past, num_segments=x.shape[0])
        flow_total = jnp.concatenate([fwd_agg, bwd_agg], axis=1)
        return _mlp(flow_total, W1n, b1n, W2n, b2n)
    edge_index = jnp.stack([src, dst])
    x = _layernorm(x + _L0_gnn_ref(x, edge_index, edge_attr_4, edge_attr_32, L0_gnn_W1, L0_gnn_b1, L0_gnn_W2, L0_gnn_b2, L0_gnn_si_w0, L0_gnn_si_w1), axis=-1)
    x = _layernorm(x + _L1_gnn_ref(x, edge_index, edge_weight1, edge_attr_3, edge_attr_5, L1_gnn_W), axis=-1)
    x = _layernorm(x + _L2_gnn_ref(x, src, dst, L2_gnn_w1_W, L2_gnn_w1_b, L2_gnn_w2_W, L2_gnn_w2_b, L2_gnn_a), axis=-1)
    x = _layernorm(x + _L3_gnn_ref(x, edge_index, edge_attr_16, L3_gnn_W1f, L3_gnn_b1f, L3_gnn_W2f, L3_gnn_b2f, L3_gnn_W1b, L3_gnn_b1b, L3_gnn_W2b, L3_gnn_b2b, L3_gnn_W1n, L3_gnn_b1n, L3_gnn_W2n, L3_gnn_b2n), axis=-1)
    return x

_drawn_inputs = setup_inputs


def setup_inputs(seed=0):
    import zlib

    import numpy as np

    out = dict(_drawn_inputs(seed))
    spreads = {'L0_gnn_b1': (0.0, 0.1),
     'L0_gnn_b2': (0.0, 0.1),
     'L3_gnn_b1f': (0.0, 0.1),
     'L3_gnn_b2f': (0.0, 0.1),
     'L3_gnn_b1b': (0.0, 0.1),
     'L3_gnn_b2b': (0.0, 0.1),
     'L3_gnn_b1n': (0.0, 0.288),
     'L3_gnn_b2n': (0.0, 0.1)}
    factors = {}
    for name, (base, spread) in spreads.items():
        noise = np.random.default_rng([zlib.crc32(name.encode()), seed]).standard_normal(out[name].shape)
        drawn = base * np.exp(spread * noise) if base else spread * noise
        out[name] = jnp.asarray(drawn.astype(out[name].dtype))
    for name, factor in factors.items():
        out[name] = (out[name] * factor).astype(out[name].dtype)
    return out
```

```python
import math
from contextlib import ExitStack

import concourse.bass as bass
from concourse import mybir

F32 = mybir.dt.float32
I32 = mybir.dt.int32
ALU = mybir.AluOpType
ACT = mybir.ActivationFunctionType
AX = mybir.AxisListType

P = 128
T = 5
E = P * T
HALF = E // 2
W = 64
RING = 4
CH = 1280
NB = CH // P
BIG = 1.0e30
EPS = 1e-5
LAYERS = 4


class Turn:

    def __init__(self, i, c, groups):
        self.i, self.c, self.groups = i, c, groups

    @property
    def g(self):
        return self.i * RING + self.c

    def near(self, d):
        return Turn(self.i, self.c + d, self.groups)

    def ring(self, layer):
        n = layer * self.groups + self.c
        slot = n % RING
        earlier = (layer * self.groups - slot + RING - 1) // RING
        return slot, self.i + n // RING, self.i + n // RING - earlier


def graph_kernel(nc, a, out):
    N = a["x"].shape[0]
    G = a["src"].shape[0] // E
    C = a["xT"].shape[1] // CH
    NT = C * CH
    NW = -(-N // W)
    NW += NW % 2
    DUMP = NT
    assert NW * W <= NT and G * E == a["src"].shape[0]

    ctx = ExitStack()
    with ctx:
        def sb(name, shape, dt=F32):
            return ctx.enter_context(nc.sbuf_tensor(name, shape, dt))

        def sem(name):
            return ctx.enter_context(nc.semaphore(name))

        def sems(name, n=RING):
            return [sem(f"{name}{i}") for i in range(n)]

        def dram(name, shape, dt=F32):
            return nc.dram_tensor(name, shape, dt, kind="Internal").ap()

        rows = [a["x"], dram("rows1", [NT, 32]), dram("rows2", [NT, 34]), dram("rows3", [NT, 32])]
        WIDTH = [32, 32, 34, 32]
        target_logit = dram("target_logit", [NT, 1])
        projected = dram("projected", [NT, P])
        back = [dram(f"back{t}", [NT + P, 32]) for t in range(T)]
        base_d = dram("base_d", [G])
        span_d = dram("span_d", [G])

        S = sb("S", [P, NT])
        AREA = max(NT, 13 * E)
        arena = sb("arena", [P, AREA])
        M = arena[0:33, 0:NT]
        used = [0]

        def part(n):
            used[0] += n
            assert used[0] <= AREA
            return arena[:, used[0] - n:used[0]]

        TA = 3 * P
        featT = part(RING * TA).rearrange("p (r e) -> p r e", r=RING)
        hidT = part(2 * E).rearrange("p (r e) -> p r e", r=2)
        pA = part(T * 128).rearrange("p (t i o) -> p t i o", t=T, i=16)
        pB = part(T * 64).rearrange("p (t i o) -> p t i o", t=T, i=8)
        pC = part(T * 192).rearrange("p (t m i o) -> p t m i o", t=T, m=3, i=8)
        used[0] = 0
        prod = part(2 * T * 248).rearrange("p (r t f) -> p r t f", r=2, t=T)
        used[0] = 0
        stack = part(RING * E).rearrange("p (r e) -> p r e", r=RING)
        src_row = part(RING * E).bitcast(I32).rearrange("p (r e) -> p r e", r=RING)
        same = part(E).rearrange("p (t e) -> p t e", t=T)
        hidden3 = part(E)
        back_in = part(T * NB * 32).rearrange("p (t b f) -> p t b f", t=T, b=NB)

        idx = sb("idx", [P, RING, T], I32)
        xs = sb("xs", [P, RING, T * 34])
        sh = sb("sh", [P, RING, T * 9])
        z = sb("z", [P, T, 16])
        vs = sb("vs", [P, T, 3, 8])
        vtmp = sb("vtmp", [P, T, 8, 3])
        mB = sb("mB", [P, T, 8])
        msg0 = sb("msg0", [P, 2, T, 56])
        onehot = sb("onehot", [P, 2, T, W])
        agg_sb = sb("agg_sb", [P, 2 * W])
        dst_row = sb("dst_row", [P, RING, E], I32)
        pen = sb("pen", [W, E])
        junk = sb("junk", [P, E])
        mcol = sb("mcol", [W, 4])
        qwin = sb("qwin", [W, RING])
        oh_r = sb("oh_r", [P, T, W])
        expo = sb("expo", [P, 3, T])
        aexp = sb("aexp", [P, T])
        val = sb("val", [P, T, 33])
        merge = sb("merge", [33, 6, W])
        first3 = sb("first3", [P, RING, P])
        back_idx = sb("back_idx", [P, RING, T], I32)
        back_tmp = sb("back_tmp", [P, 3, T])
        comb = sb("comb", [P, RING, T * 32])
        msg3 = sb("msg3", [P, T, 64])
        dst_all = sb("dst_all", [P, G * T], I32)
        rel = sb("rel", [P, G * T])
        wrel = sb("wrel", [P, T])
        node_of = sb("node_of", [P, G])
        wnode = sb("wnode", [P, 1])
        base_f = sb("base_f", [P, G])
        base_i = sb("base_i", [1, G], I32)
        narrow_i = sb("narrow_i", [1, 1], I32)
        GP = 125 if G % 125 == 0 else 1
        GA = G // GP
        span_in = pen[:, :].bitcast(I32)
        gmin = sb("gmin", [P, 3, GA])
        chunk = sb("chunk", [97, CH])
        yc = sb("yc", [P, NB, 32])
        sq = sb("sq", [P, NB, 32])
        stat = sb("stat", [P, 6, NB])
        xn = sb("xn", [P, NB, 34])
        hs = sb("hs", [P, NB, 33])
        flow_xT = sb("flow_xT", [96, CH])
        flow, xTs = flow_xT[0:64, :], flow_xT
        proj_sb = sb("proj_sb", [P, NB * P])
        nh = sb("nh", [65, CH])
        x3 = sb("x3", [P, NB, 32])
        ident = sb("ident", [P, P])
        iota = sb("iota", [P, W])
        tri = sb("tri", [P, P])
        pcol = sb("pcol", [P, 2])
        w1 = sb("w1", [64, P])
        b1 = sb("b1", [P, 1])
        w2 = sb("w2", [65, 256])
        fold0 = sb("fold0", [96, 32])
        fold1 = sb("fold1", [96, 32])
        si = sb("si", [96, 32])
        wsel_r = sb("wsel_r", [48, 4, P])
        wsel_c = sb("wsel_c", [P, 2, 4])
        wall = sb("wall", [48, 8])
        mix = sb("mix", [P, 2, 32])
        att = sb("att", [32, 33])
        a_col = sb("a_col", [32, 1])
        nu = sb("nu", [P, 33])
        lin2 = sb("lin2", [97, 32])
        proj = sb("proj", [96, P])
        rest3 = sb("rest3", [64, P])
        b13 = sb("b13", [P, 1])
        w23 = sb("w23", [P, 64])
        b23 = sb("b23", [1, 64])
        ones = sb("ones", [1, P])
        zrow = sb("zrow", [1, HALF])
        w1n = sb("w1n", [64, 64])
        b1n = sb("b1n", [64, 1])
        w2n = sb("w2n", [65, 32])
        eps = sb("eps", [P, 1])
        zeros = sb("zeros", [64, 1])

        ps = ctx.enter_context(nc.psum_tensor("ps", [P, 8 * 512], F32))

        def bank(b, n=512):
            return ps[:, b * 512:b * 512 + n]

        const_in = sem("const_in")
        const_ready = sem("const_ready")
        weights_mm = sem("weights_mm")
        zeroed = sem("zeroed")
        back_zero = sem("back_zero")
        xT_in = sem("xT_in")
        prep_in = sem("prep_in")
        prep_min = sem("prep_min")
        prep_out = sem("prep_out")
        prep_back = sem("prep_back")
        flag_ready = sem("flag_ready")
        idx_loaded = sems("idx_loaded")
        gathered = sems("gathered")
        slot_free = sems("slot_free")
        attrs = [sems(f"attrs{n}_") for n in range(LAYERS)]
        win_loaded = [sems("qwin_loaded"), sems("awin_loaded")]
        onehot_ready = sems("onehot_ready", LAYERS)
        weighed, msg3_ready = sem("weighed"), sem("msg3_ready")
        agg_mm = sems("agg_mm", LAYERS)
        added = sems("added", LAYERS)
        hid_mm, hid_act = sem("hid_mm"), sem("hid_act")
        w_mm, prods = sem("w_mm"), sem("prods")
        agg_out, mix_mm = sem("agg_out"), sem("mix_mm")
        waits_passed = sem("waits_passed")
        stack_zero, rest_mm = sem("stack_zero"), sem("rest_mm")
        logit_mm, max_ready, bcast_mm = sem("logit_mm"), sem("max_ready"), sem("bcast_mm")
        expo_ready, exp_done = sem("expo_ready"), sem("exp_done")
        diff_ready, scale_done = sem("diff_ready"), sem("scale_done")
        srcT_mm, srcT_out = sem("srcT_mm"), sem("srcT_out")
        onehotT_ready, win_mm, pre_mm, pre_act = sem("onehotT_ready"), sem("win_mm"), sem("pre_mm"), sem("pre_act")
        lin_mm, same_ready, comb_mm = sem("lin_mm"), sem("same_ready"), sem("comb_mm")
        index_ready, retired = sem("index_ready"), sem("retired")
        scattered = sems("scattered", T)
        chunk_copied, y_mm, centered, var_ready = sem("chunk_copied"), sem("y_mm"), sem("centered"), sem("var_ready")
        std_ready, xn_ready, table_written = sem("std_ready"), sem("xn_ready"), sem("table_written")
        xt_mm, xt_copied = sem("xt_mm"), sem("xt_copied")
        logit_written, proj_mm, proj_out, proj_written = sem("logit_written"), sem("proj_mm"), sem("proj_out"), sem("proj_written")
        tr_mm, hs_ready, hs_mm, hs_out = sem("tr_mm"), sem("hs_ready"), sem("hs_mm"), sem("hs_out")
        back_in_ld, back_mm, flow_ready, nh_mm, nh_ready = sem("back_in_ld"), sem("back_mm"), sem("flow_ready"), sem("nh_mm"), sem("nh_ready")
        x3_used = sem("x3_used")
        out_written = sem("out_written")

        def groups(eng, lo, hi, body):
            n = (hi - lo) // RING
            if n:
                with eng.Fori(0, n) as i:
                    for c in range(lo, lo + RING):
                        body(Turn(i, c, G))
            for g in range(lo + n * RING, hi):
                body(Turn(0, g, G))

        def windows(eng, turn, body):
            with eng.Fori(0, NW) as w:
                body(turn.g * NW + w, w * W)

        def chunks(eng, stage, body, hi=C):
            with eng.Fori(0, hi) as c:
                body(c, c + stage * C)

        def standing(eng):
            eng.sem_inc(waits_passed, 1)

        def wait_used(eng, turn, layer):
            slot, lap, _ = turn.ring(layer)
            eng.wait_ge(slot_free[slot], lap + 1)

        def steps(wide):
            return G * NW if wide else G

        block = ctx.enter_context(nc.Block())

        src_g = a["src"].rearrange("(g p t) -> g p t", p=P, t=T)
        dst_tp = a["dst_tp"].rearrange("(g e) -> g e", e=E)
        src_tp = a["src_tp"].rearrange("(g e) -> g e", e=E)

        def per_edge(name, g):
            return a[name].rearrange("(g p t) c -> g p (t c)", p=P, t=T)[bass.ds(g, 1), :, :].rearrange("o p f -> (o p) f")

        def table_rows(table, c, width):
            return table[bass.ds(c * CH, CH), 0:width].rearrange("(b p) f -> p b f", p=P)

        CONSTS = []

        def sp_program(sp, wide):
            def index_load(turn, layer):
                slot, lap, _ = turn.ring(layer)
                sp.wait_ge(gathered[slot], lap * (16 * T))
                if layer == 3:
                    sp.wait_ge(slot_free[slot], lap)
                sp.dma_start(idx[:, slot, :], src_g[bass.ds(turn.g, 1), :, :].rearrange("o p t -> (o p) t"))\
                  .then_inc(idx_loaded[slot], 16)
                sp.wait_ge(slot_free[slot], lap)
                return slot

            def layer0(turn):
                slot = index_load(turn, 0)
                sp.dma_start(featT[0:32, slot, :], a["featT"][:, bass.ds(turn.g * E, TA)]).then_inc(attrs[0][slot], 16)
                sp.dma_start(featT[32:64, slot, 0:E - TA], a["featT"][:, bass.ds(turn.g * E + TA, E - TA)])\
                  .then_inc(attrs[0][slot], 16)
                sp.dma_start(sh[:, slot, 0:T * 4], per_edge("edge_attr_4", turn.g)).then_inc(attrs[0][slot], 16)

            def layer1(turn):
                slot = index_load(turn, 1)
                sp.dma_start(sh[:, slot, 0:T], per_edge("edge_weight1", turn.g)).then_inc(attrs[1][slot], 16)
                sp.dma_start(sh[:, slot, T:4 * T], per_edge("edge_attr_3", turn.g)).then_inc(attrs[1][slot], 16)
                sp.dma_start(sh[:, slot, 4 * T:9 * T], per_edge("edge_attr_5", turn.g)).then_inc(attrs[1][slot], 16)

            def window_rows(dst, table, node, done):
                sp.dma_start(dst, table[bass.ds(node, W), :]).then_inc(done, 16)

            def layer2(turn):
                slot = index_load(turn, 2)
                sp.dma_start(dst_row[0:W, slot, :], dst_tp[bass.ds(turn.g, 1), :].to_broadcast([W, E])).then_inc(attrs[2][slot], 16)
                if not wide:
                    base = sp.value_load(base_i[0:1, bass.ds(turn.g, 1)], min_val=0, max_val=N - 1)
                    window_rows(qwin[:, slot:slot + 1], target_logit, base, win_loaded[0][slot])
                else:
                    def window(s, node):
                        sp.wait_ge(max_ready, s)
                        window_rows(qwin[:, 0:1], target_logit, node, win_loaded[0][0])
                    windows(sp, turn, window)

            def layer3(turn):
                slot = index_load(turn, 3)
                sp.dma_start(dst_row[64:128, slot, :], dst_tp[bass.ds(turn.g, 1), :].to_broadcast([W, E])).then_inc(attrs[3][slot], 16)
                sp.dma_start(src_row[:, slot, :], src_tp[bass.ds(turn.g, 1), :].to_broadcast([P, E])).then_inc(attrs[3][slot], 16)
                sp.dma_start(stack[32:48, slot, :], a["attrT"][:, bass.ds(turn.g * E, E)]).then_inc(attrs[3][slot], 16)
                if not wide:
                    base = sp.value_load(base_i[0:1, bass.ds(turn.g, 1)], min_val=0, max_val=N - 1)
                    window_rows(first3[64:128, slot, :], projected, base, win_loaded[1][slot])
                else:
                    def window(s, node):
                        sp.wait_ge(win_mm, s)
                        window_rows(first3[64:128, 0, :], projected, node, win_loaded[1][0])
                    windows(sp, turn, window)

            def store(stage):
                def body(c, n):
                    sp.wait_ge(xn_ready, n + 1)
                    sp.dma_start(table_rows(rows[stage + 1], c, WIDTH[stage + 1]), xn[:, :, 0:WIDTH[stage + 1]])\
                      .then_inc(table_written, 16)
                    if stage == 1:
                        sp.dma_start(target_logit[bass.ds(c * CH, CH), :].rearrange("(b p) o -> p (b o)", p=P), stat[:, 5, :],
                                     allow_slow_non_contiguous=True)\
                          .then_inc(logit_written, 16)
                    if stage == 2:
                        sp.wait_ge(proj_out, c + 1)
                        sp.dma_start(projected[bass.ds(c * CH, CH), :].rearrange("(b p) f -> p b f", p=P),
                                     proj_sb[:, :].rearrange("p (b f) -> p b f", b=NB)).then_inc(proj_written, 16)
                chunks(sp, stage, body)

            groups(sp, 0, G, layer0)
            store(0)
            groups(sp, 0, G, layer1)
            store(1)
            sp.wait_ge(logit_written, 16 * C)
            groups(sp, 0, G, layer2)
            store(2)
            sp.wait_ge(proj_written, 16 * C)
            sp.wait_ge(stack_zero, 1)
            groups(sp, 0, G, layer3)

            for t in range(T):
                sp.wait_ge(scattered[t], 16 * G)

            def load_back(c, n):
                sp.wait_ge(back_mm, c)
                sp.wait_ge(x3_used, c)
                for t in range(T):
                    sp.dma_start(back_in[:, t, :, :], table_rows(back[t], c, 32)).then_inc(back_in_ld, 16)
                sp.dma_start(x3[:, :, :], table_rows(rows[3], c, 32)).then_inc(back_in_ld, 16)

            def store_out(c, size):
                sp.wait_ge(xn_ready, c + 3 * C + 1)
                full = size // P
                if full:
                    sp.dma_start(out[bass.ds(c * CH, full * P), :].rearrange("(b p) f -> p b f", p=P), xn[:, 0:full, 0:32])\
                      .then_inc(out_written, 16)
                if size % P:
                    left = size % P
                    sp.dma_start(out[bass.ds(c * CH + full * P, left), :], xn[0:left, full, 0:32]).then_inc(out_written, 16)

            whole = N // CH
            if whole:
                with sp.Fori(0, whole) as c:
                    load_back(c, None)
                    store_out(c, CH)
            stores = whole
            for c in range(whole, C):
                load_back(c, None)
                size = N - c * CH
                store_out(c, size)
                stores += (size >= P) + (size % P > 0)
            sp.wait_ge(out_written, 16 * stores)

        @block.sync
        def _(sp):
            def c(dst, src, slow=False):
                CONSTS.append(1)
                sp.dma_start(dst, src, allow_slow_non_contiguous=slow).then_inc(const_in, 16)

            sp.wait_ge(zeroed, 1)
            per = (NT + P) * 32 // P
            assert per <= NT
            for t in range(T):
                sp.dma_start(back[t].rearrange("(p n) f -> p (n f)", p=P), S[:, 0:per]).then_inc(back_zero, 16)
            sp.wait_ge(const_ready, 1)
            c(ident[:, :], a["c_ident"])
            c(iota[:, :], a["c_iota"])
            c(tri[:, :], a["c_tri"])
            c(pcol[:, :], a["c_pcol"])
            c(fold0[:, :], a["c_fold0"])
            c(fold1[:, :], a["c_fold1"])
            c(wsel_r[:, :, :], a["c_wsel_r"])
            c(wsel_c[:, :, :], a["c_wsel_c"])
            for k in range(2):
                c(w1[32 * k:32 * k + 32, 64 * k:64 * k + 64], a["L0_gnn_W1"])
                c(b1[64 * k:64 * k + 64, :], a["L0_gnn_b1"])
            for to, frm in enumerate((0, 3, 1, 2)):
                c(w2[0:64, to * 64:to * 64 + 64], a["L0_gnn_W2"][:, frm * 64:frm * 64 + 64])
                c(w2[64:65, to * 64:to * 64 + 64], a["L0_gnn_b2"][:, frm * 64:frm * 64 + 64])
            c(si[64:72, 0:8], a["L0_gnn_si_w0"])
            for m in range(3):
                c(si[72 + m:96:3, 8 + m:32:3], a["L0_gnn_si_w1"], True)
            c(wall[:, :], a["L1_gnn_W"].rearrange("c i o -> (c i) o"))
            c(att[:, 0:32], a["L2_gnn_w2_W"])
            c(att[:, 32:33], a["L2_gnn_w2_b"].rearrange("a o -> o a"))
            c(a_col[:, :], a["L2_gnn_a"].rearrange("a o -> o a"))
            c(lin2[64:96, :], a["w1_WT"])
            c(lin2[96:97, :], a["L2_gnn_w1_b"])
            c(lin2[0:32, :], a["w2_WT"])
            c(lin2[32:33, :], a["L2_gnn_w2_b"])
            c(proj[64:96, 0:64], a["L3_gnn_W1f"][0:32, :])
            c(proj[64:96, 64:128], a["L3_gnn_W1b"][32:64, :])
            c(rest3[0:32, 0:64], a["L3_gnn_W1f"][32:64, :])
            c(rest3[0:32, 64:128], a["L3_gnn_W1b"][0:32, :])
            c(rest3[32:48, 0:64], a["L3_gnn_W1f"][64:80, :])
            c(rest3[32:48, 64:128], a["L3_gnn_W1b"][64:80, :])
            c(b13[0:64, :], a["L3_gnn_b1f"])
            c(b13[64:128, :], a["L3_gnn_b1b"])
            c(w23[0:64, 0:32], a["L3_gnn_W2f"])
            c(w23[64:128, 32:64], a["L3_gnn_W2b"])
            c(b23[:, 0:32], a["L3_gnn_b2f"])
            c(b23[:, 32:64], a["L3_gnn_b2b"])
            c(w1n[:, :], a["L3_gnn_W1n"])
            c(b1n[:, :], a["L3_gnn_b1n"])
            c(w2n[0:64, :], a["L3_gnn_W2n"])
            c(w2n[64:65, :], a["L3_gnn_b2n"])
            sp.dma_start(dst_all[:, :], a["dst_pg"]).then_inc(prep_in, 16)
            for k in range(GA):
                if k:
                    sp.wait_ge(prep_min, k)
                if GP <= W:
                    view = span_in[0:GP, :]
                else:
                    view = junk[0:GP, :].bitcast(I32)
                sp.dma_start(view, a["dst"].rearrange("(p k e) -> k p e", p=GP, e=E)[k, :, :]).then_inc(prep_in, 16)
            sp.wait_ge(prep_min, GA + 1)
            sp.dma_start(base_d.rearrange("(p k) -> p k", p=GP), gmin[0:GP, 0, :]).then_inc(prep_out, 16)
            sp.dma_start(span_d.rearrange("(p k) -> p k", p=GP), gmin[0:GP, 2, :]).then_inc(prep_out, 16)
            sp.wait_ge(prep_out, 32)
            sp.dma_start(base_f[:, :], base_d.rearrange("(o g) -> o g", o=1).to_broadcast([P, G])).then_inc(prep_back, 16)
            sp.dma_start(junk[0:1, 0:G], span_d.rearrange("(o g) -> o g", o=1)).then_inc(prep_back, 16)
            sp.wait_ge(back_zero, 16 * T)
            sp.dma_start(S[64:96, :], a["xT"]).then_inc(xT_in, 16)
            sp.wait_ge(flag_ready, 1)
            is_wide = sp.value_load(narrow_i[0:1, 0:1], min_val=0, max_val=1)
            with sp.If(is_wide == 0):
                sp_program(sp, False)
            with sp.Else():
                sp_program(sp, True)

        def pool_program(pool, wide):
            def gather(layer):
                def body(turn):
                    slot, lap, _ = turn.ring(layer)
                    pool.wait_ge(idx_loaded[slot], lap * 16 + 16)
                    pool.wait_ge(slot_free[slot], lap)
                    standing(pool)
                    w = WIDTH[layer]
                    for t in range(T):
                        pool.indirect_dma_start(xs[:, slot, t * w:(t + 1) * w], None, rows[layer][:, :],
                                                bass.IndirectOffsetOnAxis(ap=idx[:, slot, t:t + 1], axis=0))\
                            .then_inc(gathered[slot], 16)
                return body

            def scatter(turn):
                for t in range(T):
                    pool.wait_ge(scattered[t], turn.g * 16)
                pool.wait_ge(index_ready, turn.g + 1)
                wait_used(pool, turn, 3)
                pool.sem_inc(retired, 1)
                slot = turn.ring(3)[0]
                for t in range(T):
                    pool.indirect_dma_start(back[t][:, :], bass.IndirectOffsetOnAxis(ap=back_idx[:, slot, t:t + 1], axis=0),
                                            comb[:, slot, t * 32:(t + 1) * 32], None, compute_op=ALU.add)\
                        .then_inc(scattered[t], 16)

            for layer in range(3):
                if layer:
                    pool.wait_ge(table_written, 16 * C * layer)
                groups(pool, 0, G, gather(layer))
            pool.wait_ge(table_written, 16 * C * 3)
            pool.wait_ge(back_zero, 16 * T)
            pool.sem_inc(retired, RING - 2)
            lead = 2
            for g in range(lead):
                gather(3)(Turn(0, g, G))

            def both(turn):
                gather(3)(turn.near(lead))
                scatter(turn)
            groups(pool, 0, G - lead, both)
            for g in range(G - lead, G):
                scatter(Turn(0, g, G))

        @block.gpsimd
        def _(pool):
            pool.memset(S[:, :], 0.0).then_inc(zeroed, 1)
            pool.wait_ge(flag_ready, 1)
            is_wide = pool.value_load(narrow_i[0:1, 0:1], min_val=0, max_val=1)
            with pool.If(is_wide == 0):
                pool_program(pool, False)
            with pool.Else():
                pool_program(pool, True)

        def pe_program(pe, wide):
            hid_ps = [bank(0, TA), bank(1, TA)]
            w_ps = ps[:, 2 * 512:5 * 512]
            agg0_ps = bank(5)[0:56, 0:W]

            def hidden0(turn):
                slot, _, local = turn.ring(0)
                pe.wait_ge(attrs[0][slot], local * 48 + 48)
                pe.wait_ge(hid_act, turn.g * 2)
                pe.matmul(hid_ps[turn.c % 2], w1[:, :], featT[0:64, slot, :], start=True, stop=True).then_inc(hid_mm, 1)

            def weights0(turn, first=False):
                for j, tiles in enumerate(((0, 1), (2, 3), (4,))):
                    pe.wait_ge(hid_act, turn.g * 2 + (2 if j == 2 or tiles[-1] > 2 else 1))
                    if not first:
                        pe.wait_ge(prods, turn.g * 3 + (j - 2))
                    for t in tiles:
                        last = pe.matmul(w_ps[:, t * 256:(t + 1) * 256], hidT[0:65, turn.c % 2, t * P:(t + 1) * P],
                                         w2[:, :], start=True, stop=True)
                    last.then_inc(w_mm, 1)

            def agg0(turn, s, slot, oh):
                wait_used(pe, turn, 0)
                pe.wait_ge(onehot_ready[0], s + 1)
                pe.wait_ge(added[0], s)
                for t in range(T):
                    last = pe.matmul(agg0_ps, msg0[:, slot, t, :], onehot[:, oh, t, :], start=(t == 0), stop=(t == T - 1))
                last.then_inc(agg_mm[0], 1)

            if not wide:
                t0 = Turn(0, 0, G)
                hidden0(t0)
                hidden0(t0.near(1))
                weights0(t0, True)

                def body(turn):
                    hidden0(turn.near(1))
                    weights0(turn)
                    p = turn.near(-1)
                    agg0(p, p.g, p.c % 2, p.c % 2)
                groups(pe, 1, G - 1, body)
                last = Turn(0, G - 1, G)
                weights0(last)
                for t in (last.near(-1), last):
                    agg0(t, t.g, t.c % 2, t.c % 2)
            else:
                def body(turn, first=False):
                    hidden0(turn)
                    weights0(turn, first)
                    windows(pe, turn, lambda s, node: agg0(turn, s, turn.c % 2, 0))
                body(Turn(0, 0, G), True)
                groups(pe, 1, G, body)

            y_ps = bank(7)[:, 0:NB * 32]
            xt_ps = ps[:, 4 * 512:4 * 512 + CH]

            def to_features(n):
                pe.wait_ge(xn_ready, n + 1)
                pe.wait_ge(xt_copied, n)
                for b in range(NB):
                    last = pe.matmul(xt_ps[64:96, b * P:(b + 1) * P], xn[:, b, 0:32], ident[:, :], start=True, stop=True)
                last.then_inc(xt_mm, 1)

            def fold(weights):
                def body(c, n):
                    pe.wait_ge(chunk_copied, n + 1)
                    pe.wait_ge(centered, n)
                    for b in range(NB):
                        last = pe.matmul(y_ps[:, b * 32:(b + 1) * 32], chunk[0:96, b * P:(b + 1) * P], weights[:, :],
                                         start=True, stop=True)
                    last.then_inc(y_mm, 1)
                    to_features(n)
                return body
            chunks(pe, 0, fold(fold0))

            agg1_ps = [bank(0)[:, 0:W], bank(1)[0:120, 0:W]]
            mix_ps = bank(2)[0:32, 0:W]

            def agg1(turn, s, slot, oh):
                wait_used(pe, turn, 1)
                pe.wait_ge(onehot_ready[1], s + 1)
                pe.wait_ge(agg_out, s)
                for k, (lo, hi) in enumerate(((0, 128), (128, 248))):
                    for t in range(T):
                        last = pe.matmul(agg1_ps[k], prod[:, slot, t, lo:hi], onehot[:, oh, t, :], start=(t == 0), stop=(t == T - 1))
                last.then_inc(agg_mm[1], 1)

            def mix1(s):
                pe.wait_ge(agg_out, s + 1)
                pe.wait_ge(added[1], s)
                pe.matmul(mix_ps, mix[:, 0, :], agg_sb[:, 0:W], start=True, stop=False)
                pe.matmul(mix_ps, mix[0:120, 1, :], agg_sb[0:120, W:2 * W], start=False, stop=True).then_inc(mix_mm, 1)

            if not wide:
                agg1(Turn(0, 0, G), 0, 0, 0)

                def body(turn):
                    mix1(turn.near(-1).g)
                    agg1(turn, turn.g, turn.c % 2, turn.c % 2)
                groups(pe, 1, G, body)
                mix1(G - 1)
            else:
                def body(turn):
                    def window(s, node):
                        agg1(turn, s, turn.c % 2, 0)
                        mix1(s)
                    windows(pe, turn, window)
                groups(pe, 0, G, body)
            chunks(pe, 1, fold(fold1))

            logit_ps = [ps[:, 0:2 * 512], ps[:, 6 * 512:8 * 512]]
            r_ps = bank(2)[:, 0:W]
            m_ps = [bank(3)[0:33, 0:W], bank(4)[0:33, 0:W]]
            att_ps = bank(5)[0:33, 0:W]

            def logits(turn, s, buf, free):
                slot, lap, _ = turn.ring(2)
                pe.wait_ge(gathered[slot], lap * (16 * T) + 16 * T)
                if free is not None:
                    pe.wait_ge(max_ready, free)
                for t in range(T):
                    last = pe.matmul(logit_ps[buf][0:W, t * P:(t + 1) * P],
                                     xs[:, slot, t * 34 + 33:t * 34 + 34].to_broadcast([P, W]), ident[:, :], start=True, stop=True)
                last.then_inc(logit_mm, 1)

            def spread_max(s, mslot):
                pe.wait_ge(max_ready, s + 1)
                pe.matmul(r_ps, mcol[:, 2:3].to_broadcast([W, P]), ident[0:W, 0:W], start=True, stop=True)
                pe.matmul(m_ps[mslot], mcol[:, 1:2].to_broadcast([W, 33]), ident[0:W, 0:W], start=True, stop=True)\
                  .then_inc(bcast_mm, 1)

            def attend(s):
                pe.wait_ge(weighed, s + 1)
                pe.wait_ge(added[2], s)
                for t in range(T):
                    last = pe.matmul(att_ps, val[:, t, :], onehot[:, 0, t, :], start=(t == 0), stop=(t == T - 1))
                last.then_inc(agg_mm[2], 1)

            if not wide:
                logits(Turn(0, 0, G), 0, 0, None)

                def body(turn):
                    spread_max(turn.g, turn.c % 2)
                    nxt = turn.near(1)
                    logits(nxt, nxt.g, nxt.c % 2, turn.g)
                    attend(turn.g)
                groups(pe, 0, G - 1, body)
                spread_max(G - 1, (G - 1) % 2)
                attend(G - 1)
            else:
                def body(turn):
                    def window(s, node):
                        logits(turn, s, 0, s)
                        spread_max(s, 0)
                        attend(s)
                    windows(pe, turn, window)
                groups(pe, 0, G, body)

            mid_ps = ps[:, 512:512 + CH]

            def attention_nodes(c, n):
                pe.wait_ge(chunk_copied, n + 1)
                pe.wait_ge(hs_ready, c)
                for b in range(NB):
                    last = pe.matmul(bank(0)[:, b * 33:(b + 1) * 33], chunk[0:33, b * P:(b + 1) * P], ident[0:33, 0:33],
                                     start=True, stop=True)
                last.then_inc(tr_mm, 1)
                pe.wait_ge(hs_ready, c + 1)
                pe.wait_ge(proj_out, c)
                for b in range(NB):
                    last = pe.matmul(mid_ps[0:33, b * P:(b + 1) * P], hs[:, b, :], ident[:, :], start=True, stop=True)
                last.then_inc(hs_mm, 1)
                pe.wait_ge(hs_out, c + 1)
                pe.wait_ge(centered, n)
                for b in range(NB):
                    last = pe.matmul(y_ps[:, b * 32:(b + 1) * 32], chunk[0:97, b * P:(b + 1) * P], lin2[:, :],
                                     start=True, stop=True)
                last.then_inc(y_mm, 1)
                to_features(n)
                pe.wait_ge(xt_copied, n + 1)
                for b in range(NB):
                    last = pe.matmul(mid_ps[:, b * P:(b + 1) * P], xTs[64:96, b * P:(b + 1) * P], proj[64:96, :],
                                     start=True, stop=True)
                last.then_inc(proj_mm, 1)
            chunks(pe, 2, attention_nodes)

            srcT_ps = ps[:, 0:2 * 512]
            pre_ps = [bank(2, HALF), bank(3, HALF)]
            lin_ps = bank(4)[:, 0:T * 64]
            comb_ps = bank(5)[:, 0:T * 32]
            fwd_ps = bank(6)[0:32, 0:W]

            def srcT(turn):
                slot, lap, _ = turn.ring(3)
                pe.wait_ge(gathered[slot], lap * (16 * T) + 16 * T)
                pe.wait_ge(srcT_out, turn.g)
                for t in range(T):
                    last = pe.transpose(srcT_ps[0:32, t * P:(t + 1) * P], xs[:, slot, t * 32:(t + 1) * 32], ident[:, :])
                last.then_inc(srcT_mm, 1)

            def pre(turn):
                slot, lap, local = turn.ring(3)
                pe.wait_ge(srcT_out, turn.g + 1)
                pe.wait_ge(attrs[3][slot], local * 48 + 48)
                pe.wait_ge(stack_zero, 1)
                pe.wait_ge(pre_act, turn.g * 2)
                if not wide:
                    pe.wait_ge(onehotT_ready, turn.g + 1)
                    pe.wait_ge(win_loaded[1][slot], local * 16 + 16)
                if not wide:
                    for h in range(2):
                        pe.matmul(pre_ps[h], first3[:, slot, :], stack[:, slot, h * HALF:(h + 1) * HALF],
                                  start=True, stop=True).then_inc(pre_mm, 1)
                else:
                    for h in range(2):
                        last = pe.matmul(pre_ps[h], first3[:, 1, :], stack[:, slot, h * HALF:(h + 1) * HALF],
                                         start=True, stop=False)
                    last.then_inc(rest_mm, 1)

                    def window(s, node):
                        pe.wait_ge(onehotT_ready, s + 1)
                        pe.wait_ge(win_loaded[1][0], s * 16 + 16)
                        for h in range(2):
                            last = pe.matmul(pre_ps[h], first3[:, 0, :], stack[:, slot, h * HALF:(h + 1) * HALF],
                                             start=False, stop=False)
                        last.then_inc(win_mm, 1)
                    windows(pe, turn, window)
                    for h in range(2):
                        pe.matmul(pre_ps[h], ones[:, :], zrow[:, :], start=False, stop=True).then_inc(pre_mm, 1)

            def second(turn):
                pe.wait_ge(pre_act, turn.g * 2 + 2)
                pe.wait_ge(msg3_ready, turn.g)
                for t in range(T):
                    pe.matmul(lin_ps[:, t * 64:(t + 1) * 64], hidden3[:, t * P:(t + 1) * P], w23[:, :], start=True, stop=False)
                    last = pe.matmul(lin_ps[:, t * 64:(t + 1) * 64], ones[:, :], b23[:, :], start=False, stop=True)
                last.then_inc(lin_mm, 1)

            def fwd_agg(turn, s):
                pe.wait_ge(onehot_ready[3], s + 1)
                pe.wait_ge(added[3], s)
                for t in range(T):
                    last = pe.matmul(fwd_ps, msg3[:, t, 0:32], onehot[:, 0, t, :], start=(t == 0), stop=(t == T - 1))
                last.then_inc(agg_mm[3], 1)

            def combine(turn):
                pe.wait_ge(msg3_ready, turn.g + 1)
                wait_used(pe, turn.near(-1), 3)
                standing(pe)
                if not wide:
                    fwd_agg(turn, turn.g)
                else:
                    windows(pe, turn, lambda s, node: fwd_agg(turn, s))
                pe.wait_ge(same_ready, turn.g + 1)
                for t in range(T):
                    last = pe.matmul(comb_ps[:, t * 32:(t + 1) * 32], same[:, t, :], msg3[:, t, 32:64], start=True, stop=True)
                last.then_inc(comb_mm, 1)

            t0 = Turn(0, 0, G)
            srcT(t0)

            def body(turn):
                pre(turn)
                srcT(turn.near(1))
                second(turn)
                combine(turn)
            groups(pe, 0, G - 1, body)
            last = Turn(0, G - 1, G)
            pre(last)
            second(last)
            combine(last)

            def flow_nodes(c, n):
                pe.wait_ge(back_in_ld, c * (16 * (T + 1)) + 16 * (T + 1))
                pe.wait_ge(flow_ready, c)
                for b in range(NB):
                    for t in range(T):
                        last = pe.matmul(mid_ps[32:64, b * P:(b + 1) * P], back_in[:, t, b, :], ident[:, :],
                                         start=(t == 0), stop=(t == T - 1))
                last.then_inc(back_mm, 1)
                pe.wait_ge(flow_ready, c + 1)
                pe.wait_ge(nh_ready, c)
                standing(pe)
                for lo in range(0, CH, 512):
                    hi = min(lo + 512, CH)
                    last = pe.matmul(xt_ps[0:64, lo:hi], w1n[:, :], flow[:, lo:hi], start=True, stop=True)
                last.then_inc(nh_mm, 1)
                pe.wait_ge(nh_ready, c + 1)
                pe.wait_ge(centered, n)
                for b in range(NB):
                    last = pe.matmul(y_ps[:, b * 32:(b + 1) * 32], nh[:, b * P:(b + 1) * P], w2n[:, :], start=True, stop=True)
                last.then_inc(y_mm, 1)
            chunks(pe, 3, flow_nodes)

        @block.tensor
        def _(pe):
            pe.wait_ge(const_in, 16 * len(CONSTS))
            pe.wait_ge(const_ready, 2)
            for k in range(4):
                last = pe.matmul(bank(0)[:, k * 8:k * 8 + 8], wsel_r[:, k, :], wall[:, :], start=True, stop=True)
            pe.matmul(bank(1)[:, 0:33], a_col[:, 0:1].to_broadcast([32, P]), att[:, :], start=True, stop=True)\
              .then_inc(weights_mm, 1)
            pe.wait_ge(const_ready, 3)
            pe.wait_ge(flag_ready, 1)
            is_wide = pe.value_load(narrow_i[0:1, 0:1], min_val=0, max_val=1)
            with pe.If(is_wide == 0):
                pe_program(pe, False)
            with pe.Else():
                pe_program(pe, True)

        def act_program(act, wide):
            mid_ps = ps[:, 512:512 + CH]
            xt_ps = ps[:, 4 * 512:4 * 512 + CH]

            def relu0(turn):
                act.wait_ge(hid_mm, turn.g + 1)
                hid = bank(turn.c % 2, TA)
                act.activation(hidT[0:64, turn.c % 2, 0:TA], hid[0:64, :], ACT.Relu, bias=b1[0:64, :]).then_inc(hid_act, 1)
                act.activation(hidT[0:64, turn.c % 2, TA:E], hid[64:128, 0:E - TA], ACT.Relu, bias=b1[64:128, :])\
                   .then_inc(hid_act, 1)
            groups(act, 0, G, relu0)

            def copy_chunk(c, n, top):
                act.wait_ge(y_mm, n)
                act.activation(chunk[0:top, :], S[0:top, bass.ds(c * CH, CH)], ACT.Copy).then_inc(chunk_copied, 1)

            def std(n):
                act.wait_ge(var_ready, n + 1)
                act.activation(stat[:, 2, :], stat[:, 1, :], ACT.Sqrt, bias=eps[:, :], scale=1.0 / 32).then_inc(std_ready, 1)

            def features(c, n, extra=False):
                act.wait_ge(xt_mm, n + 1)
                if extra:
                    act.wait_ge(proj_mm, c)
                    act.activation(xTs[64:96, :], xt_ps[64:96, :], ACT.Copy)
                act.activation(S[64:96, bass.ds(c * CH, CH)], xt_ps[64:96, :], ACT.Copy).then_inc(xt_copied, 1)

            def simple(layer):
                def body(c, n):
                    copy_chunk(c, n, 96)
                    std(n)
                    features(c, n)
                act.wait_ge(added[layer], steps(wide))
                chunks(act, layer, body)
            act.wait_ge(xT_in, 16)
            simple(0)

            def out1(s):
                act.wait_ge(agg_mm[1], s + 1)
                act.wait_ge(mix_mm, s)
                act.activation(agg_sb[:, 0:W], bank(0)[:, 0:W], ACT.Copy)
                act.activation(agg_sb[0:120, W:2 * W], bank(1)[0:120, 0:W], ACT.Copy).then_inc(agg_out, 1)

            def body(turn):
                if not wide:
                    out1(turn.g)
                else:
                    windows(act, turn, lambda s, node: out1(s))
            groups(act, 0, G, body)
            simple(1)

            def exp_edges(s):
                act.wait_ge(expo_ready, s + 1)
                act.wait_ge(weighed, s)
                act.activation(aexp[:, :], expo[:, 1, :], ACT.Exp).then_inc(exp_done, 1)

            def exp_scales(s):
                act.wait_ge(diff_ready, s + 1)
                act.activation(merge[:, 3:5, :], merge[:, 1:3, :], ACT.Exp).then_inc(scale_done, 1)

            if not wide:
                exp_edges(0)

                def body(turn):
                    exp_scales(turn.near(-1).g)
                    exp_edges(turn.g)
                groups(act, 1, G, body)
                exp_scales(G - 1)
            else:
                def body(turn):
                    def window(s, node):
                        exp_edges(s)
                        exp_scales(s)
                    windows(act, turn, window)
                groups(act, 0, G, body)

            def attention_nodes(c, n):
                copy_chunk(c, n, 96)
                act.wait_ge(hs_mm, c + 1)
                act.activation(chunk[0:33, :], mid_ps[0:33, :], ACT.Copy).then_inc(hs_out, 1)
                std(n)
                features(c, n, True)
                act.wait_ge(proj_mm, c + 1)
                act.wait_ge(proj_written, c * 16)
                act.activation(proj_sb[:, :], mid_ps, ACT.Copy).then_inc(proj_out, 1)
            act.wait_ge(added[2], steps(wide))
            chunks(act, 2, attention_nodes)

            def srcT(turn):
                slot, lap, _ = turn.ring(3)
                act.wait_ge(srcT_mm, turn.g + 1)
                act.wait_ge(slot_free[slot], lap)
                act.activation(stack[0:32, slot, :], ps[0:32, 0:E], ACT.Copy).then_inc(srcT_out, 1)

            def relu3(turn):
                act.wait_ge(lin_mm, turn.g)
                for h in range(2):
                    act.wait_ge(pre_mm, turn.g * 2 + h + 1)
                    act.activation(hidden3[:, h * HALF:(h + 1) * HALF], bank(2 + h, HALF), ACT.Relu, bias=b13[:, :])\
                       .then_inc(pre_act, 1)

            def relu_out(turn):
                act.wait_ge(lin_mm, turn.g + 1)
                act.wait_ge(comb_mm, turn.g)
                act.activation(msg3[:, :, :], bank(4)[:, 0:T * 64], ACT.Relu).then_inc(msg3_ready, 1)

            def comb_out(turn):
                act.wait_ge(comb_mm, turn.g + 1)
                act.wait_ge(index_ready, turn.g + 1)
                act.wait_ge(retired, turn.g)
                slot = turn.ring(3)[0]
                act.activation(comb[:, slot, :], bank(5)[:, 0:T * 32], ACT.Copy).then_inc(slot_free[slot], 1)

            act.wait_ge(stack_zero, 1)
            srcT(Turn(0, 0, G))

            def body(turn):
                relu3(turn)
                srcT(turn.near(1))
                relu_out(turn)
                comb_out(turn)
            groups(act, 0, G - 1, body)
            last = Turn(0, G - 1, G)
            relu3(last)
            relu_out(last)
            comb_out(last)

            def flow_nodes(c, n):
                act.wait_ge(back_mm, c + 1)
                act.wait_ge(nh_mm, c)
                act.activation(flow[0:32, :], S[0:32, bass.ds(c * CH, CH)], ACT.Copy)
                act.activation(flow[32:64, :], mid_ps[32:64, :], ACT.Copy).then_inc(flow_ready, 1)
                act.wait_ge(nh_mm, c + 1)
                act.wait_ge(y_mm, n)
                act.activation(nh[0:64, :], xt_ps[0:64, :], ACT.Relu, bias=b1n[:, :]).then_inc(nh_ready, 1)
                std(n)
            act.wait_ge(added[3], steps(wide))
            chunks(act, 3, flow_nodes)

        @block.scalar
        def _(act):
            act.wait_ge(const_in, 16 * len(CONSTS))
            act.wait_ge(const_ready, 3)
            act.wait_ge(flag_ready, 1)
            is_wide = act.value_load(narrow_i[0:1, 0:1], min_val=0, max_val=1)
            with act.If(is_wide == 0):
                act_program(act, False)
            with act.Else():
                act_program(act, True)

        def dve_program(v, wide):
            def rel_of(turn):
                return rel[:, bass.ds(turn.g * T, T)]

            def one_hot(slot, r):
                return v.tensor_tensor(onehot[:, slot, :, :], iota[:, :].unsqueeze(1).to_broadcast([P, T, W]),
                                       r.unsqueeze(2).to_broadcast([P, T, W]), ALU.is_equal)

            def base_of(g):
                return v.value_load(base_i[0:1, bass.ds(g, 1)], min_val=0, max_val=N - 1)

            def add(layer, s, node, rows_, psum, done=None):
                v.wait_ge(agg_mm[layer] if done is None else done, s + 1)
                win = S[0:rows_, bass.ds(node, W)]
                v.tensor_tensor(win, psum, win, ALU.add).then_inc(added[layer], 1)
                v.drain()

            def wide_start(turn):
                v.tensor_copy(wrel[:, :], rel_of(turn))
                v.tensor_copy(wnode[:, :], pcol[:, 0:1])
                v.drain()

            def wide_next():
                v.drain()
                v.tensor_scalar(wrel[:, :], wrel[:, :], -float(W), None, ALU.add)
                v.tensor_scalar(wnode[:, :], wnode[:, :], float(W), None, ALU.add)
                v.drain()

            w_ps = ps[:, 2 * 512:5 * 512].rearrange("p (t f) -> p t f", f=256)

            def products0(turn, first=False):
                slot, lap, local = turn.ring(0)
                v.wait_ge(gathered[slot], lap * (16 * T) + 16 * T)
                v.wait_ge(attrs[0][slot], local * 48 + 48)
                x = xs[:, slot, 0:T * 32].rearrange("p (t f) -> p t f", t=T)
                h = sh[:, slot, 0:T * 4].rearrange("p (t f) -> p t f", t=T)
                vec = x[:, :, 8:32].rearrange("p t (i m) -> p t i m", m=3)
                v.tensor_tensor(z[:, :, 0:8], x[:, :, 0:8], h[:, :, 0:1].to_broadcast([P, T, 8]), ALU.mult)
                v.tensor_tensor(vtmp[:, :, :, :], vec, h[:, :, 1:4].unsqueeze(2).to_broadcast([P, T, 8, 3]), ALU.mult)
                v.tensor_tensor(vs[:, :, :, :], vec.rearrange("p t i m -> p t m i"),
                                h[:, :, 0:1].unsqueeze(3).to_broadcast([P, T, 3, 8]), ALU.mult)
                v.drain()
                v.tensor_reduce(z[:, :, 8:16], vtmp[:, :, :, :], AX.X, ALU.add)
                v.drain()
                for j, (lo, hi) in enumerate(((0, 2), (2, 4), (4, 5))):
                    n = hi - lo
                    v.wait_ge(w_mm, turn.g * 3 + j + 1)
                    v.tensor_tensor(pA[:, lo:hi, :, :], w_ps[:, lo:hi, 0:128].rearrange("p t (i o) -> p t i o", o=8),
                                    z[:, lo:hi, :].unsqueeze(3).to_broadcast([P, n, 16, 8]), ALU.mult)
                    v.tensor_tensor(pB[:, lo:hi, :, :], w_ps[:, lo:hi, 128:192].rearrange("p t (i o) -> p t i o", o=8),
                                    x[:, lo:hi, 0:8].unsqueeze(3).to_broadcast([P, n, 8, 8]), ALU.mult)
                    v.tensor_tensor(pC[:, lo:hi, :, :, :],
                                    w_ps[:, lo:hi, 192:256].rearrange("p t (i o) -> p t i o", o=8).unsqueeze(2)
                                    .to_broadcast([P, n, 3, 8, 8]),
                                    vs[:, lo:hi, :, :].unsqueeze(4).to_broadcast([P, n, 3, 8, 8]), ALU.mult)\
                     .then_inc(prods, 1)
                v.drain()
                if wide:
                    v.wait_ge(agg_mm[0], turn.g * NW)
                elif not first:
                    v.wait_ge(agg_mm[0], turn.g - 1)
                msg = msg0[:, turn.c % 2, :, :]
                v.tensor_reduce(msg[:, :, 0:8], pA[:, :, :, :].rearrange("p t i o -> p t o i"), AX.X, ALU.add)
                v.tensor_reduce(mB[:, :, :], pB[:, :, :, :].rearrange("p t i o -> p t o i"), AX.X, ALU.add)
                v.tensor_reduce(msg[:, :, 32:56].rearrange("p t (m o) -> p t m o", m=3),
                                pC[:, :, :, :, :].rearrange("p t m i o -> p t m o i"), AX.X, ALU.add)
                v.drain()
                last = v.tensor_tensor(msg[:, :, 8:32].rearrange("p t (o m) -> p t o m", m=3),
                                       mB[:, :, :].unsqueeze(3).to_broadcast([P, T, 8, 3]),
                                       h[:, :, 1:4].unsqueeze(2).to_broadcast([P, T, 8, 3]), ALU.mult)
                last.then_inc(slot_free[slot], 1)

            agg0_ps = bank(5)[0:56, 0:W]

            def narrow_onehot(layer, turn, first=False):
                if not first:
                    v.wait_ge(agg_mm[layer], turn.g - 1)
                one_hot(turn.c % 2, rel_of(turn)).then_inc(onehot_ready[layer], 1)

            if not wide:
                t0 = Turn(0, 0, G)
                narrow_onehot(0, t0, True)
                products0(t0, True)

                def body(turn):
                    narrow_onehot(0, turn)
                    products0(turn)
                    p = turn.near(-1).g
                    add(0, p, base_of(p), 56, agg0_ps)
                groups(v, 1, G, body)
                add(0, G - 1, base_of(G - 1), 56, agg0_ps)
            else:
                def body(turn):
                    products0(turn)
                    wide_start(turn)

                    def window(s, node):
                        one_hot(0, wrel[:, :]).then_inc(onehot_ready[0], 1)
                        add(0, s, node, 56, agg0_ps)
                        wide_next()
                    windows(v, turn, window)
                groups(v, 0, G, body)

            y_ps = bank(7)[:, 0:NB * 32].rearrange("p (b f) -> p b f", b=NB)

            def clear(c, n):
                v.wait_ge(chunk_copied, n + 1)
                v.tensor_scalar(S[0:64, bass.ds(c * CH, CH)], zeros[:, :].to_broadcast([64, CH]), 0.0, None, ALU.add)

            def layer_norm(n, y):
                v.tensor_reduce(stat[:, 0, :], y, AX.X, ALU.add)
                v.drain()
                v.tensor_scalar(stat[:, 3, :], stat[:, 0, :], -1.0 / 32, None, ALU.mult)
                v.drain()
                v.tensor_tensor(yc[:, :, :], y, stat[:, 3, :].unsqueeze(2).to_broadcast([P, NB, 32]), ALU.add).then_inc(centered, 1)
                v.drain()
                v.tensor_tensor(sq[:, :, :], yc[:, :, :], yc[:, :, :], ALU.mult)
                v.drain()
                v.tensor_reduce(stat[:, 1, :], sq[:, :, :], AX.X, ALU.add).then_inc(var_ready, 1)
                v.wait_ge(std_ready, n + 1)
                v.reciprocal(stat[:, 4, :], stat[:, 2, :])
                v.drain()

            def normalized():
                return v.tensor_tensor(xn[:, :, 0:32], yc[:, :, :], stat[:, 4, :].unsqueeze(2).to_broadcast([P, NB, 32]), ALU.mult)

            def free_xn(c, n):
                v.wait_ge(table_written, n * 16)
                v.wait_ge(xt_mm, n)

            def plain_nodes(c, n):
                clear(c, n)
                v.wait_ge(y_mm, n + 1)
                layer_norm(n, y_ps)
                free_xn(c, n)
                normalized().then_inc(xn_ready, 1)
                v.drain()
            chunks(v, 0, plain_nodes)

            def products1(turn, first=False):
                slot, lap, local = turn.ring(1)
                v.wait_ge(gathered[slot], lap * (16 * T) + 16 * T)
                v.wait_ge(attrs[1][slot], local * 48 + 48)
                if wide:
                    v.wait_ge(agg_mm[1], turn.g * NW)
                elif not first:
                    v.wait_ge(agg_mm[1], turn.g - 1)
                x = xs[:, slot, 0:T * 32].rearrange("p (t f) -> p t f", t=T)
                pr = prod[:, turn.c % 2, :, :]
                v.tensor_tensor(pr[:, :, 0:32], x, sh[:, slot, 0:T].unsqueeze(2).to_broadcast([P, T, 32]), ALU.mult)
                v.tensor_tensor(pr[:, :, 32:128].rearrange("p t (k f) -> p t k f", k=3), x.unsqueeze(2).to_broadcast([P, T, 3, 32]),
                                sh[:, slot, T:4 * T].rearrange("p (t k) -> p t k", t=T).unsqueeze(3).to_broadcast([P, T, 3, 32]),
                                ALU.mult)
                last = v.tensor_tensor(pr[:, :, 128:248].rearrange("p t (k f) -> p t k f", k=5),
                                       x[:, :, 8:32].unsqueeze(2).to_broadcast([P, T, 5, 24]),
                                       sh[:, slot, 4 * T:9 * T].rearrange("p (t k) -> p t k", t=T).unsqueeze(3)
                                       .to_broadcast([P, T, 5, 24]), ALU.mult)
                last.then_inc(slot_free[slot], 1)

            mix_ps = bank(2)[0:32, 0:W]
            if not wide:
                narrow_onehot(1, Turn(0, 0, G), True)
                products1(Turn(0, 0, G), True)

                def body(turn):
                    narrow_onehot(1, turn)
                    products1(turn)
                    p = turn.near(-1).g
                    add(1, p, base_of(p), 32, mix_ps, mix_mm)
                groups(v, 1, G, body)
                add(1, G - 1, base_of(G - 1), 32, mix_ps, mix_mm)
            else:
                def body(turn):
                    products1(turn)
                    wide_start(turn)

                    def window(s, node):
                        one_hot(0, wrel[:, :]).then_inc(onehot_ready[1], 1)
                        add(1, s, node, 32, mix_ps, mix_mm)
                        wide_next()
                    windows(v, turn, window)
                groups(v, 0, G, body)

            def attention_input(c, n):
                clear(c, n)
                v.wait_ge(y_mm, n + 1)
                layer_norm(n, y_ps)
                free_xn(c, n)
                v.wait_ge(logit_written, c * 16)
                normalized()
                v.drain()
                v.tensor_tensor(sq[:, :, :], xn[:, :, 0:32], nu[:, 0:32].unsqueeze(1).to_broadcast([P, NB, 32]), ALU.mult)
                v.drain()
                v.tensor_reduce(xn[:, :, 33:34], sq[:, :, :], AX.X, ALU.add)
                v.drain()
                v.tensor_scalar(stat[:, 5, :].unsqueeze(2), xn[:, :, 33:34], -1.0, nu[:, 32:33], ALU.mult, ALU.add).then_inc(xn_ready, 1)
                v.drain()
            chunks(v, 1, attention_input)

            v.memset(M, -BIG)
            v.drain()
            logit_ps = [ps[0:W, 0:E], ps[0:W, 6 * 512:6 * 512 + E]]
            r_ps = bank(2)[:, 0:W]
            m_ps = [bank(3)[0:33, 0:W], bank(4)[0:33, 0:W]]
            att_ps = bank(5)[0:33, 0:W]

            def local_max(turn, s, node_col, qslot, qcount, frees=None):
                slot, lap, local = turn.ring(2)
                v.wait_ge(attrs[2][slot], local * 16 + 16)
                v.tensor_scalar(pen[:, :], dst_row[0:W, slot, :], node_col, -BIG, ALU.not_equal, ALU.mult)
                waited = v.drain()
                if frees is not None:
                    waited.then_inc(slot_free[frees.ring(2)[0]], 1)
                v.wait_ge(logit_mm, s + 1)
                standing(v)
                v.tensor_tensor_reduce(out=junk[0:W, :], in0=pen[:, :], in1=logit_ps[0 if wide else turn.c % 2], scale=1.0, scalar=-BIG, op0=ALU.add,
                                       op1=ALU.max, accum_out=mcol[:, 0:1])
                v.drain()
                v.wait_ge(win_loaded[0][qslot], qcount)
                v.wait_ge(bcast_mm, s)
                v.tensor_tensor(mcol[:, 1:2], mcol[:, 0:1], qwin[:, qslot:qslot + 1], ALU.add)
                v.drain()
                v.tensor_tensor(mcol[:, 2:3], qwin[:, qslot:qslot + 1], mcol[:, 1:2], ALU.subtract).then_inc(max_ready, 1)

            def exponents(turn, s):
                slot, _, _ = turn.ring(2)
                x = xs[:, slot, :].rearrange("p (t f) -> p t f", t=T)
                v.wait_ge(bcast_mm, s + 1)
                v.tensor_tensor(oh_r[:, :, :], r_ps.unsqueeze(1).to_broadcast([P, T, W]), onehot[:, 0, :, :], ALU.mult)
                v.drain()
                v.tensor_reduce(expo[:, 0, :], oh_r[:, :, :], AX.X, ALU.add)
                v.drain()
                v.wait_ge(exp_done, s)
                if not wide:
                    v.tensor_tensor(expo[:, 1, :].unsqueeze(2), expo[:, 0, :].unsqueeze(2), x[:, :, 33:34], ALU.add)\
                     .then_inc(expo_ready, 1)
                else:
                    v.tensor_tensor(expo[:, 2, :].unsqueeze(2), expo[:, 0, :].unsqueeze(2), x[:, :, 33:34], ALU.add)
                    v.drain()
                    v.tensor_scalar(expo[:, 1, :], expo[:, 2, :], 1.0, None, ALU.min).then_inc(expo_ready, 1)

            def weigh(turn, s):
                slot, _, _ = turn.ring(2)
                x = xs[:, slot, :].rearrange("p (t f) -> p t f", t=T)
                v.wait_ge(exp_done, s + 1)
                v.wait_ge(agg_mm[2], s)
                last = v.tensor_tensor(val[:, :, :], x[:, :, 0:33], aexp[:, :].unsqueeze(2).to_broadcast([P, T, 33]), ALU.mult)
                last.then_inc(weighed, 1)

            def merge_max(s, mslot, node):
                v.wait_ge(bcast_mm, s + 1)
                v.tensor_tensor(merge[:, 0, :], m_ps[mslot], M[:, bass.ds(node, W)], ALU.max)
                v.drain()
                v.tensor_tensor(merge[:, 1, :], M[:, bass.ds(node, W)], merge[:, 0, :], ALU.subtract)
                v.tensor_tensor(merge[:, 2, :], m_ps[mslot], merge[:, 0, :], ALU.subtract)
                v.drain().then_inc(diff_ready, 1)
                v.tensor_copy(M[:, bass.ds(node, W)], merge[:, 0, :])

            def merge_sums(s, node):
                v.wait_ge(scale_done, s + 1)
                v.wait_ge(agg_mm[2], s + 1)
                win = S[0:33, bass.ds(node, W)]
                v.tensor_tensor(merge[:, 5, :], win, merge[:, 3, :], ALU.mult)
                v.tensor_tensor(merge[:, 1, :], att_ps, merge[:, 4, :], ALU.mult)
                v.drain()
                v.tensor_tensor(win, merge[:, 5, :], merge[:, 1, :], ALU.add).then_inc(added[2], 1)
                v.drain()

            if not wide:
                def front(turn, frees=None):
                    slot, _, local = turn.ring(2)
                    local_max(turn, turn.g, node_of[0:W, bass.ds(turn.g, 1)], slot, local * 16 + 16, frees)
                    v.wait_ge(agg_mm[2], turn.g)
                    one_hot(0, rel_of(turn)).then_inc(onehot_ready[2], 1)
                    v.drain()
                t0 = Turn(0, 0, G)
                front(t0)
                exponents(t0, 0)
                weigh(t0, 0)

                def body(turn):
                    p = turn.near(-1)
                    front(turn, p)
                    node = base_of(p.g)
                    merge_max(p.g, p.c % 2, node)
                    exponents(turn, turn.g)
                    merge_sums(p.g, node)
                    weigh(turn, turn.g)
                groups(v, 1, G, body)
                v.drain().then_inc(slot_free[Turn(0, G - 1, G).ring(2)[0]], 1)
                node = base_of(G - 1)
                merge_max(G - 1, (G - 1) % 2, node)
                merge_sums(G - 1, node)
            else:
                def body(turn):
                    wide_start(turn)

                    def window(s, node):
                        local_max(turn, s, wnode[0:W, :], 0, s * 16 + 16)
                        one_hot(0, wrel[:, :]).then_inc(onehot_ready[2], 1)
                        v.drain()
                        exponents(turn, s)
                        weigh(turn, s)
                        merge_max(s, 0, node)
                        merge_sums(s, node)
                        wide_next()
                    windows(v, turn, window)
                    v.drain().then_inc(slot_free[turn.ring(2)[0]], 1)
                groups(v, 0, G, body)

            def attention_nodes(c, n):
                clear(c, n)
                sums = bank(0)[:, 0:NB * 33].rearrange("p (b f) -> p b f", b=NB)
                v.wait_ge(tr_mm, c + 1)
                v.tensor_scalar(stat[:, 3, :].unsqueeze(2), sums[:, :, 32:33], 1.0e-30, None, ALU.max)
                v.drain()
                v.reciprocal(stat[:, 4, :], stat[:, 3, :])
                v.drain()
                v.wait_ge(hs_mm, c)
                v.tensor_tensor(hs[:, :, :], sums, stat[:, 4, :].unsqueeze(2).to_broadcast([P, NB, 33]), ALU.mult).then_inc(hs_ready, 1)
                v.drain()
                v.wait_ge(y_mm, n + 1)
                layer_norm(n, y_ps)
                free_xn(c, n)
                normalized().then_inc(xn_ready, 1)
                v.drain()
            chunks(v, 2, attention_nodes)

            v.memset(stack[:, :, :], 0.0)
            for slot in ((1,) if wide else range(RING)):
                v.tensor_copy(first3[0:64, slot, :], rest3[:, :])
            v.drain().then_inc(stack_zero, 1)

            def target_onehot(turn, s, node_col):
                slot, _, local = turn.ring(3)
                v.wait_ge(attrs[3][slot], local * 48 + 48)
                if wide:
                    v.wait_ge(rest_mm, turn.g + 1)
                    v.wait_ge(win_mm, s)
                v.tensor_scalar(stack[64:128, slot, :], dst_row[64:128, slot, :], node_col, None, ALU.is_equal)\
                 .then_inc(onehotT_ready, 1)

            def same_source(turn):
                slot, lap, _ = turn.ring(3)
                v.wait_ge(comb_mm, turn.g)
                v.wait_ge(idx_loaded[slot], lap * 16 + 16)
                v.tensor_tensor(same[:, :, :], src_row[:, slot, :].rearrange("p (t e) -> p t e", t=T),
                                idx[:, slot, :].unsqueeze(2).to_broadcast([P, T, P]), ALU.is_equal).then_inc(same_ready, 1)
                v.tensor_scalar(back_tmp[:, 1, :], idx[:, slot, :], -1.0, pcol[:, 1:2], ALU.mult, ALU.add)
                v.drain()
                for t in range(T):
                    v.tensor_tensor_reduce(out=junk[:, t * P:(t + 1) * P], in0=same[:, t, :], in1=tri[:, :], scale=1.0, scalar=0.0,
                                           op0=ALU.mult, op1=ALU.add, accum_out=back_tmp[:, 0, t:t + 1])
                v.drain()
                v.scalar_tensor_tensor(back_tmp[:, 2, :], back_tmp[:, 0, :], 0.5, back_tmp[:, 1, :], ALU.is_gt, ALU.mult)
                v.drain()
                v.wait_ge(retired, turn.g)
                v.tensor_tensor(back_idx[:, slot, :], back_tmp[:, 2, :], idx[:, slot, :], ALU.add).then_inc(index_ready, 1)

            fwd_ps = bank(6)[0:32, 0:W]

            def onehot3(turn):
                v.wait_ge(agg_mm[3], turn.g)
                one_hot(0, rel_of(turn)).then_inc(onehot_ready[3], 1)
                v.drain()

            if not wide:
                def front3(turn):
                    target_onehot(turn, turn.g, node_of[64:128, bass.ds(turn.g, 1)])
                    same_source(turn)
                    onehot3(turn)
                front3(Turn(0, 0, G))

                def body(turn):
                    front3(turn)
                    p = turn.near(-1).g
                    add(3, p, base_of(p), 32, fwd_ps)
                groups(v, 1, G, body)
                add(3, G - 1, base_of(G - 1), 32, fwd_ps)
            else:
                def body(turn):
                    wide_start(turn)

                    def window(s, node):
                        target_onehot(turn, s, wnode[64:128, :])
                        wide_next()
                    windows(v, turn, window)
                    same_source(turn)
                    wide_start(turn)

                    def window(s, node):
                        v.wait_ge(agg_mm[3], s)
                        one_hot(0, wrel[:, :]).then_inc(onehot_ready[3], 1)
                        add(3, s, node, 32, fwd_ps)
                        wide_next()
                    windows(v, turn, window)
                groups(v, 0, G, body)

            def flow_nodes(c, n):
                v.wait_ge(y_mm, n + 1)
                v.wait_ge(back_in_ld, c * (16 * (T + 1)) + 16 * (T + 1))
                v.scalar_tensor_tensor(sq[:, :, :], y_ps, 0.0, x3[:, :, :], ALU.max, ALU.add).then_inc(x3_used, 1)
                v.drain()
                layer_norm(n, sq[:, :, :])
            whole = N // CH

            def finish(c, stored):
                flow_nodes(c, c + 3 * C)
                v.wait_ge(out_written, stored * 16)
                normalized().then_inc(xn_ready, 1)
                v.drain()
            if whole:
                with v.Fori(0, whole) as c:
                    finish(c, c)
            stored = whole
            for c in range(whole, C):
                finish(c, stored)
                size = N - c * CH
                stored += (size >= P) + (size % P > 0)

        @block.vector
        def _(v):
            for t, x in ((chunk[96:97, :], 1.0), (nh[64:65, :], 1.0), (si[:, :], 0.0), (w23[:, :], 0.0), (lin2[:, :], 0.0), (ones[:, :], 1.0),
                         (zrow[:, :], 0.0), (w1[:, :], 0.0), (featT[:, :, :], 0.0), (rest3[:, :], 0.0), (first3[:, :, :], 0.0), (eps[:, :], EPS), (zeros[:, :], 0.0), (hidT[64:65, :, :], 1.0)):
                v.memset(t, x)
            v.drain().then_inc(const_ready, 1)
            v.memset(xn[:, :, 32:33], 1.0)
            v.memset(xs[:, :, :], 0.0)
            v.drain().then_inc(const_ready, 1)
            v.wait_ge(const_in, 16 * len(CONSTS))
            v.tensor_scalar(w2[:, 64:128], w2[:, 64:128], 1.0 / math.sqrt(3.0), None, ALU.mult)
            v.scalar_tensor_tensor(fold0[64:96, :], si[64:96, :], 1.0 / math.sqrt(8.0), fold0[64:96, :], ALU.mult, ALU.add)
            v.tensor_tensor(lin2[64:96, :], lin2[64:96, :], fold1[64:96, :], ALU.add)
            v.wait_ge(weights_mm, 1)
            for k in range(2):
                v.tensor_scalar(mix[:, k, 0:8], bank(0)[:, 16 * k:16 * k + 8], wsel_c[:, k, 0:1], None, ALU.mult)
                for m in range(3):
                    v.tensor_scalar(mix[:, k, 8 + m:32:3], bank(0)[:, 16 * k + 8:16 * k + 16], wsel_c[:, k, 1 + m:2 + m],
                                    None, ALU.mult)
            v.tensor_scalar(nu[:, 0:32], bank(1)[:, 0:32], -1.0, None, ALU.mult)
            v.tensor_copy(nu[:, 32:33], bank(1)[:, 32:33])
            v.drain().then_inc(const_ready, 1)
            for k in range(GA):
                v.wait_ge(prep_in, 16 * (k + 2))
                view = span_in[0:GP, :] if GP <= W else junk[0:GP, :].bitcast(I32)
                v.tensor_reduce(gmin[0:GP, 0, k:k + 1], view, AX.X, ALU.min)
                v.tensor_reduce(gmin[0:GP, 1, k:k + 1], view, AX.X, ALU.max)
                v.drain().then_inc(prep_min, 1)
            v.tensor_tensor(gmin[0:GP, 2, :], gmin[0:GP, 1, :], gmin[0:GP, 0, :], ALU.subtract)
            v.drain().then_inc(prep_min, 1)
            v.wait_ge(prep_back, 32)
            v.tensor_reduce(stat[0:1, 0, 0:1], junk[0:1, 0:G], AX.X, ALU.max)
            v.tensor_copy(base_i[:, :], base_f[0:1, :])
            v.tensor_scalar(node_of[:, :], base_f[:, :], pcol[:, 0:1], None, ALU.add)
            v.drain()
            v.tensor_scalar(narrow_i[:, :], stat[0:1, 0, 0:1], float(W) - 0.5, None, ALU.is_gt)
            v.drain().then_inc(flag_ready, 1)
            is_wide = v.value_load(narrow_i[0:1, 0:1], min_val=0, max_val=1)
            with v.If(is_wide == 0):
                v.tensor_tensor(rel[:, :].rearrange("p (g t) -> p g t", t=T), dst_all[:, :].rearrange("p (g t) -> p g t", t=T),
                                base_f[:, :].unsqueeze(2).to_broadcast([P, G, T]), ALU.subtract)
                v.drain()
                dve_program(v, False)
            with v.Else():
                v.tensor_copy(rel[:, :], dst_all[:, :])
                v.drain()
                dve_program(v, True)

def _cg_tables():
    import numpy as np
    f = math.factorial

    def coeff(j1, m1, j2, m2, j3, m3):
        if m3 != m1 + m2:
            return 0.0
        pref = (2 * j3 + 1) * f(j3 + j1 - j2) * f(j3 - j1 + j2) * f(j1 + j2 - j3) / f(j1 + j2 + j3 + 1)
        pref *= f(j3 + m3) * f(j3 - m3) * f(j1 - m1) * f(j1 + m1) * f(j2 - m2) * f(j2 + m2)
        s = 0.0
        for v in range(max(0, j2 - j3 - m1, j1 + m2 - j3), min(j1 + j2 - j3, j1 - m1, j2 + m2) + 1):
            s += (-1) ** v / (f(v) * f(j1 + j2 - j3 - v) * f(j1 - m1 - v) * f(j2 + m2 - v)
                              * f(j3 - j2 + m1 + v) * f(j3 - j1 - m2 + v))
        return math.sqrt(pref) * s

    def q(l):
        m_ = np.zeros((2 * l + 1, 2 * l + 1), np.complex128)
        for m in range(-l, 0):
            m_[l + m, l + abs(m)] = 1 / np.sqrt(2)
            m_[l + m, l - abs(m)] = -1j / np.sqrt(2)
        m_[l, l] = 1.0
        for m in range(1, l + 1):
            m_[l + m, l + abs(m)] = (-1) ** m / np.sqrt(2)
            m_[l + m, l - abs(m)] = 1j * (-1) ** m / np.sqrt(2)
        return (-1j) ** l * m_

    out = []
    for l1, l2, l3 in ((0, 0, 0), (0, 1, 1), (1, 0, 1), (1, 1, 0), (1, 1, 1), (2, 1, 1)):
        c = np.zeros((2 * l1 + 1, 2 * l2 + 1, 2 * l3 + 1), np.complex128)
        for m1 in range(-l1, l1 + 1):
            for m2 in range(-l2, l2 + 1):
                if -l3 <= m1 + m2 <= l3:
                    c[m1 + l1, m2 + l2, m1 + m2 + l3] = coeff(l1, m1, l2, m2, l3, m1 + m2)
        c = np.einsum("ij,kl,mn,ikn->jlm", q(l1), q(l2), np.conj(q(l3)).T, c).real
        out.append(c / np.linalg.norm(c))
    return out


def _constants():
    import numpy as np
    f32 = np.float32
    c = {"c_ident": np.eye(P, dtype=f32), "c_iota": np.tile(np.arange(W, dtype=f32), (P, 1))}
    c["c_tri"] = np.tril(np.ones((P, P), f32), -1)
    fold0 = np.zeros((96, 32), f32)
    fold0[0:32, :] = 0.25 * np.eye(32, dtype=f32)
    for m in range(3):
        for o in range(8):
            fold0[32 + m * 8 + o, 8 + o * 3 + m] = 0.25
    fold0[64:96] = np.eye(32)
    fold1 = np.zeros((96, 32), f32)
    fold1[0:32] = np.eye(32)
    fold1[64:96] = np.eye(32)
    c["c_fold0"], c["c_fold1"] = fold0, fold1
    cg = _cg_tables()
    pick = np.zeros((48, 4, P), f32)
    coef = np.zeros((P, 2, 4), f32)
    for chunk in range(2):
        for r in range(P if chunk == 0 else 120):
            if chunk == 0:
                k, f = divmod(r, 32)
            else:
                k, f = 4 + r // 24, 8 + r % 24
            scalar = f < 8
            ch, j = (f, 0) if scalar else divmod(f - 8, 3)
            i = 0 if k == 0 else k - 1 if k < 4 else k - 4
            zero = {True: 0, False: None}[scalar] if k == 0 else (3 if (k < 4 and not scalar) else None)
            one = (None if scalar else 1) if k == 0 else (2 if scalar else 4) if k < 4 else 5
            if zero is not None:
                pick[zero * 8 + ch, 2 * chunk, r] = 1
                coef[r, chunk, 0] = cg[zero][i, j, 0]
            if one is not None:
                pick[one * 8 + ch, 2 * chunk + 1, r] = 1
                coef[r, chunk, 1:4] = cg[one][i, j, :]
    c["c_wsel_r"], c["c_wsel_c"] = pick, coef
    return c


def kernel(**inputs):
    import numpy as np
    import concourse.bacc as _bacc
    from concourse.bass_utils import run_bass_kernel_spmd as _run

    given = {k: np.ascontiguousarray(v) for k, v in inputs.items()}
    n = given["x"].shape[0]
    e = given["src"].shape[0]
    g = e // E
    nt = -(-(n + W) // CH) * CH
    c = _constants()
    c["c_pcol"] = np.stack([np.arange(P) % W, nt + np.arange(P)], 1).astype(np.float32)
    arrays = dict(c)
    for k in ("x", "src", "dst", "edge_attr_4", "edge_attr_3", "edge_attr_5", "edge_weight1", "L0_gnn_W1", "L0_gnn_W2",
              "L0_gnn_si_w0", "L0_gnn_si_w1", "L1_gnn_W", "L2_gnn_w2_W", "L2_gnn_a", "L3_gnn_W1f", "L3_gnn_W1b",
              "L3_gnn_W2f", "L3_gnn_W2b", "L3_gnn_W1n", "L3_gnn_W2n"):
        arrays[k] = given[k]
    for k in ("L0_gnn_b1", "L3_gnn_b1f", "L3_gnn_b1b", "L3_gnn_b1n"):
        arrays[k] = given[k].reshape(-1, 1)
    for k in ("L0_gnn_b2", "L2_gnn_w1_b", "L2_gnn_w2_b", "L3_gnn_b2f", "L3_gnn_b2b", "L3_gnn_b2n"):
        arrays[k] = given[k].reshape(1, -1)
    def tiled(v):
        return v.reshape(g, P, T, -1).transpose(3, 0, 2, 1).reshape(-1, e)
    arrays["featT"] = np.ascontiguousarray(tiled(given["edge_attr_32"]))
    arrays["attrT"] = np.ascontiguousarray(tiled(given["edge_attr_16"]))
    arrays["dst_tp"] = np.ascontiguousarray(tiled(given["dst"]).reshape(-1))
    arrays["src_tp"] = np.ascontiguousarray(tiled(given["src"]).reshape(-1))
    arrays["dst_pg"] = np.ascontiguousarray(given["dst"].reshape(g, P, T).transpose(1, 0, 2).reshape(P, g * T))
    arrays["w1_WT"] = np.ascontiguousarray(given["L2_gnn_w1_W"].T)
    arrays["w2_WT"] = np.ascontiguousarray(given["L2_gnn_w2_W"].T)
    xt = np.zeros((32, nt), np.float32)
    xt[:, :n] = given["x"].T
    arrays["xT"] = xt

    nc = _bacc.Bacc("TRN2", target_bir_lowering=False, num_devices=1)
    a = {k: nc.dram_tensor(f"in_{k}", v.shape, mybir.dt.from_np(v.dtype), kind="ExternalInput").ap()
         for k, v in arrays.items()}
    out = nc.dram_tensor("out_x", [n, 32], F32, kind="ExternalOutput").ap()
    graph_kernel(nc, a, out)
    r = _run(nc, [{f"in_{k}": v for k, v in arrays.items()}], core_ids=[0])
    return r.results[0]["out_x"]
```

```python
import math
from contextlib import ExitStack

import concourse.bass as bass
from concourse import mybir

F32 = mybir.dt.float32
I32 = mybir.dt.int32
ALU = mybir.AluOpType
ACT = mybir.ActivationFunctionType
AX = mybir.AxisListType

P = 128
T = 5
E = P * T
HALF = E // 2
W = 64
RING = 4
CH = 1280
NB = CH // P
BIG = 1.0e30
STEEP = 2.0 ** 50
EPS = 1e-5
LAYERS = 4


class Turn:

    def __init__(self, i, c, groups):
        self.i, self.c, self.groups = i, c, groups

    @property
    def g(self):
        return self.i * RING + self.c

    def near(self, d):
        return Turn(self.i, self.c + d, self.groups)

    def ring(self, layer):
        n = layer * self.groups + self.c
        slot = n % RING
        earlier = (layer * self.groups - slot + RING - 1) // RING
        return slot, self.i + n // RING, self.i + n // RING - earlier


def graph_kernel(nc, a, out):
    N = a["x"].shape[0]
    G = a["src"].shape[0] // E
    C = a["xT"].shape[1] // CH
    NT = C * CH
    NW = -(-N // W)
    NW += NW % 2
    DUMP = NT
    assert NW * W <= NT and (NT * STEEP) ** 2 < 3.4e38 and G * E == a["src"].shape[0]

    ctx = ExitStack()
    with ctx:
        def sb(name, shape, dt=F32):
            return ctx.enter_context(nc.sbuf_tensor(name, shape, dt))

        def sem(name):
            return ctx.enter_context(nc.semaphore(name))

        def sems(name, n=RING):
            return [sem(f"{name}{i}") for i in range(n)]

        counting = []

        def counter(name):
            counting.append(sem(name))
            return counting[-1]

        def counters(name, n=RING):
            return [counter(f"{name}{i}") for i in range(n)]

        def past(n):
            return n + 1

        def dram(name, shape, dt=F32):
            return nc.dram_tensor(name, shape, dt, kind="Internal").ap()

        rows = [a["x"], dram("rows1", [NT, 32]), dram("rows2", [NT, 34]), dram("rows3", [NT, 32])]
        WIDTH = [32, 32, 34, 32]
        target_logit = dram("target_logit", [NT, 1])
        projected = dram("projected", [NT, P])
        back = [dram(f"back{t}", [NT + P, 32]) for t in range(T)]
        base_d = dram("base_d", [G])
        span_d = dram("span_d", [G])

        S = sb("S", [P, NT])
        AREA = max(NT, 13 * E)
        arena = sb("arena", [P, AREA])
        M = arena[0:33, 0:NT]
        used = [0]

        def part(n):
            used[0] += n
            assert used[0] <= AREA
            return arena[:, used[0] - n:used[0]]

        featT = part(RING * HALF).rearrange("p (r e) -> p r e", r=RING)
        hidT = part(2 * E).rearrange("p (r e) -> p r e", r=2)
        pA = part(T * 128).rearrange("p (t i o) -> p t i o", t=T, i=16)
        pB = part(T * 64).rearrange("p (t i o) -> p t i o", t=T, i=8)
        pC = part(T * 192).rearrange("p (t m i o) -> p t m i o", t=T, m=3, i=8)
        apart = part(T * W).rearrange("p (t w) -> p t w", t=T)
        sums0 = part(RING * W)[0:56, :].rearrange("p (r w) -> p r w", r=RING)
        used[0] = 0
        prod = part(2 * T * 248).rearrange("p (r t f) -> p r t f", r=2, t=T)
        used[0] = 0
        stack = part(RING * E).rearrange("p (r e) -> p r e", r=RING)
        src_row = part(RING * E).bitcast(I32).rearrange("p (r e) -> p r e", r=RING)
        same = part(E).rearrange("p (t e) -> p t e", t=T)
        hidden3 = part(E)
        back_in = part(T * NB * 32).rearrange("p (t b f) -> p t b f", t=T, b=NB)

        idx = sb("idx", [P, RING, T], I32)
        xs = sb("xs", [P, RING, T * 34])
        sh = sb("sh", [P, RING, T * 9])
        z = sb("z", [P, 2, T, 16])
        vs = sb("vs", [P, 2, T, 24])
        vtmp = sb("vtmp", [P, T, 8, 3])
        mB = sb("mB", [P, T, 8])
        msg0 = sb("msg0", [P, 2, T, 56])
        onehot = sb("onehot", [P, 2, T, W])
        agg_sb = sb("agg_sb", [P, 2 * W])
        dst_row = sb("dst_row", [P, RING, E], I32)
        pen = sb("pen", [W, E])
        junk = sb("junk", [P, E])
        mcol = sb("mcol", [W, 4])
        qwin = sb("qwin", [W, RING])
        oh_r = sb("oh_r", [P, T, W])
        expo = sb("expo", [P, 3, T])
        aexp = sb("aexp", [P, T])
        val = sb("val", [P, T, 33])
        merge = sb("merge", [33, 6, W])
        first3 = sb("first3", [P, RING, P])
        back_idx = sb("back_idx", [P, RING, T], I32)
        back_tmp = sb("back_tmp", [P, 3, T])
        comb = sb("comb", [P, RING, T * 32])
        msg3 = sb("msg3", [P, T, 64])
        dst_all = sb("dst_all", [P, G * T], I32)
        rel = sb("rel", [P, G * T])
        wrel = sb("wrel", [P, T])
        node_of = sb("node_of", [P, G])
        node_steep = sb("node_steep", [W, G])
        wnode = sb("wnode", [P, 1])
        base_f = sb("base_f", [P, G])
        base_i = sb("base_i", [1, G], I32)
        narrow_i = sb("narrow_i", [1, 1], I32)
        GP = 125 if G % 125 == 0 else 1
        GA = G // GP
        span_in = pen[:, :].bitcast(I32)
        gmin = sb("gmin", [P, 3, GA])
        chunk = sb("chunk", [97, CH])
        yc = sb("yc", [P, NB, 32])
        sq = sb("sq", [P, NB, 32])
        stat = sb("stat", [P, 6, NB])
        xn = sb("xn", [P, NB, 34])
        hs = sb("hs", [P, NB, 33])
        flow_xT = sb("flow_xT", [96, CH])
        flow, xTs = flow_xT[0:64, :], flow_xT
        proj_sb = sb("proj_sb", [P, NB * P])
        nh = sb("nh", [65, CH])
        x3 = sb("x3", [P, NB, 32])
        ident = sb("ident", [P, P])
        iota = sb("iota", [P, W])
        tri = sb("tri", [P, P])
        pcol = sb("pcol", [P, 2])
        w1 = sb("w1", [64, P])
        b1 = sb("b1", [P, 1])
        w2 = sb("w2", [65, 256])
        fold0 = sb("fold0", [96, 32])
        fold1 = sb("fold1", [96, 32])
        si = sb("si", [96, 32])
        wsel_r = sb("wsel_r", [48, 4, P])
        wsel_c = sb("wsel_c", [P, 2, 4])
        wall = sb("wall", [48, 8])
        mix = sb("mix", [P, 2, 32])
        att = sb("att", [32, 33])
        a_col = sb("a_col", [32, 1])
        nu = sb("nu", [P, 33])
        lin2 = sb("lin2", [97, 32])
        proj = sb("proj", [96, P])
        rest3 = sb("rest3", [64, P])
        b13 = sb("b13", [P, 1])
        w23 = sb("w23", [P, 64])
        b23 = sb("b23", [1, 64])
        ones = sb("ones", [1, P])
        zrow = sb("zrow", [1, HALF])
        w1n = sb("w1n", [64, 64])
        b1n = sb("b1n", [64, 1])
        w2n = sb("w2n", [65, 32])
        eps = sb("eps", [P, 1])
        unit = sb("unit", [P, 1])
        zeros = sb("zeros", [64, 1])

        ps = ctx.enter_context(nc.psum_tensor("ps", [P, 8 * 512], F32))

        def bank(b, n=512):
            return ps[:, b * 512:b * 512 + n]

        const_in = sem("const_in")
        const_ready = sem("const_ready")
        weights_mm = sem("weights_mm")
        zeroed = sem("zeroed")
        back_zero = sem("back_zero")
        xT_in = sem("xT_in")
        prep_in = sem("prep_in")
        prep_min = sem("prep_min")
        prep_out = sem("prep_out")
        prep_back = sem("prep_back")
        flag_ready = sem("flag_ready")
        rel_ready = sem("rel_ready")
        sums_out = counter("sums_out")
        idx_loaded = sems("idx_loaded")
        gathered = sems("gathered")
        slot_free = counters("slot_free")
        attrs = [sems(f"attrs{n}_") for n in range(LAYERS)]
        win_loaded = [sems("qwin_loaded"), sems("awin_loaded")]
        onehot_ready = sems("onehot_ready", LAYERS)
        weighed, msg3_ready = counter("weighed"), counter("msg3_ready")
        agg_mm = counters("agg_mm", LAYERS)
        added = counters("added", LAYERS)
        scaled = sem("scaled")
        hid_mm, hid_act = sem("hid_mm"), counter("hid_act")
        w_mm, prods = sem("w_mm"), sem("prods")
        agg_out, mix_mm = counter("agg_out"), counter("mix_mm")
        waits_passed = sem("waits_passed")
        stack_zero = sem("stack_zero")
        rest_mm = sem("rest_mm")
        logit_mm, max_ready, bcast_mm = sem("logit_mm"), counter("max_ready"), counter("bcast_mm")
        pen_ready = sem("pen_ready")
        expo_ready, exp_done = sem("expo_ready"), counter("exp_done")
        diff_ready, scale_done = sem("diff_ready"), sem("scale_done")
        srcT_mm, srcT_out = sem("srcT_mm"), counter("srcT_out")
        onehotT_ready, win_mm, pre_mm, pre_act = sem("onehotT_ready"), counter("win_mm"), sem("pre_mm"), counter("pre_act")
        lin_mm, same_ready, comb_mm = counter("lin_mm"), sem("same_ready"), counter("comb_mm")
        index_ready, retired = sem("index_ready"), counter("retired")
        scattered = sems("scattered", T)
        chunk_copied, y_mm, centered, var_ready = sem("chunk_copied"), counter("y_mm"), counter("centered"), sem("var_ready")
        std_ready, xn_ready, table_written = sem("std_ready"), sem("xn_ready"), counter("table_written")
        xt_mm, xt_copied = counter("xt_mm"), counter("xt_copied")
        logit_written, proj_mm, proj_out, proj_written = counter("logit_written"), counter("proj_mm"), counter("proj_out"), counter("proj_written")
        tr_mm, hs_ready, hs_mm, hs_out = sem("tr_mm"), counter("hs_ready"), counter("hs_mm"), sem("hs_out")
        back_in_ld, back_mm, flow_ready, nh_mm, nh_ready = sem("back_in_ld"), counter("back_mm"), counter("flow_ready"), counter("nh_mm"), counter("nh_ready")
        x3_in, x3_used = sem("x3_in"), counter("x3_used")
        out_written = counter("out_written")

        def groups(eng, lo, hi, body):
            n = (hi - lo) // RING
            if n:
                with eng.Fori(0, n) as i:
                    for c in range(lo, lo + RING):
                        body(Turn(i, c, G))
            for g in range(lo + n * RING, hi):
                body(Turn(0, g, G))

        def windows(eng, turn, body):
            with eng.Fori(0, NW) as w:
                body(turn.g * NW + w, w * W)

        def chunks(eng, stage, body, hi=C):
            if hi:
                with eng.Fori(0, hi) as c:
                    body(c, c + stage * C)

        def standing(eng):
            eng.sem_inc(waits_passed, 1)

        def wait_used(eng, turn, layer):
            slot, lap, _ = turn.ring(layer)
            eng.wait_ge(slot_free[slot], past(lap + 1))

        def steps(wide):
            return G * NW if wide else G

        block = ctx.enter_context(nc.Block())

        src_g = a["src"].rearrange("(g p t) -> g p t", p=P, t=T)
        dst_tp = a["dst_tp"].rearrange("(g e) -> g e", e=E)
        src_tp = a["src_tp"].rearrange("(g e) -> g e", e=E)

        def per_edge(name, g):
            return a[name].rearrange("(g p t) c -> g p (t c)", p=P, t=T)[bass.ds(g, 1), :, :].rearrange("o p f -> (o p) f")

        def table_rows(table, c, width):
            return table[bass.ds(c * CH, CH), 0:width].rearrange("(b p) f -> p b f", p=P)

        CONSTS = []

        def sp_program(sp, wide):
            def index_load(turn, layer, first=False):
                slot, lap, _ = turn.ring(layer)
                if not first:
                    sp.wait_ge(gathered[slot], lap * (16 * T))
                    standing(sp)
                if layer == 3:
                    sp.wait_ge(slot_free[slot], past(lap))
                sp.dma_start(idx[:, slot, :], src_g[bass.ds(turn.g, 1), :, :].rearrange("o p t -> (o p) t"))\
                  .then_inc(idx_loaded[slot], 16)
                sp.wait_ge(slot_free[slot], past(lap))
                return slot

            def layer0(turn, first=False):
                slot = index_load(turn, 0, first)
                sp.dma_start(featT[0:32, slot, :], a["featT"][:, bass.ds(turn.g * E, HALF)]).then_inc(attrs[0][slot], 16)
                sp.dma_start(featT[32:64, slot, :], a["featT"][:, bass.ds(turn.g * E + HALF, HALF)])\
                  .then_inc(attrs[0][slot], 16)
                sp.dma_start(sh[:, slot, 0:T * 4], per_edge("edge_attr_4", turn.g)).then_inc(attrs[0][slot], 16)

            def layer1(turn):
                slot = index_load(turn, 1)
                sp.dma_start(sh[:, slot, 0:T], per_edge("edge_weight1", turn.g)).then_inc(attrs[1][slot], 16)
                sp.dma_start(sh[:, slot, T:4 * T], per_edge("edge_attr_3", turn.g)).then_inc(attrs[1][slot], 16)
                sp.dma_start(sh[:, slot, 4 * T:9 * T], per_edge("edge_attr_5", turn.g)).then_inc(attrs[1][slot], 16)

            def window_rows(dst, table, node, done):
                sp.dma_start(dst, table[bass.ds(node, W), :]).then_inc(done, 16)

            def layer2(turn):
                slot = index_load(turn, 2)
                sp.dma_start(dst_row[0:W, slot, :], dst_tp[bass.ds(turn.g, 1), :].to_broadcast([W, E])).then_inc(attrs[2][slot], 16)
                if not wide:
                    base = sp.value_load(base_i[0:1, bass.ds(turn.g, 1)], min_val=0, max_val=N - 1)
                    window_rows(qwin[:, slot:slot + 1], target_logit, base, win_loaded[0][slot])
                else:
                    def window(s, node):
                        sp.wait_ge(max_ready, past(s))
                        window_rows(qwin[:, 0:1], target_logit, node, win_loaded[0][0])
                    windows(sp, turn, window)

            def layer3(turn):
                slot = index_load(turn, 3)
                sp.dma_start(dst_row[64:128, slot, :], dst_tp[bass.ds(turn.g, 1), :].to_broadcast([W, E])).then_inc(attrs[3][slot], 16)
                sp.dma_start(src_row[:, slot, :], src_tp[bass.ds(turn.g, 1), :].to_broadcast([P, E])).then_inc(attrs[3][slot], 16)
                sp.dma_start(stack[32:48, slot, :], a["attrT"][:, bass.ds(turn.g * E, E)]).then_inc(attrs[3][slot], 16)
                if not wide:
                    base = sp.value_load(base_i[0:1, bass.ds(turn.g, 1)], min_val=0, max_val=N - 1)
                    window_rows(first3[64:128, slot, :], projected, base, win_loaded[1][slot])
                else:
                    def window(s, node):
                        sp.wait_ge(win_mm, past(s))
                        window_rows(first3[64:128, 0, :], projected, node, win_loaded[1][0])
                    windows(sp, turn, window)

            def store(stage):
                def body(c, n):
                    sp.wait_ge(xn_ready, n + 1)
                    sp.dma_start(table_rows(rows[stage + 1], c, WIDTH[stage + 1]), xn[:, :, 0:WIDTH[stage + 1]])\
                      .then_inc(table_written, 16)
                    if stage == 1:
                        sp.dma_start(target_logit[bass.ds(c * CH, CH), :].rearrange("(b p) o -> p (b o)", p=P), stat[:, 5, :],
                                     allow_slow_non_contiguous=True)\
                          .then_inc(logit_written, 16)
                    if stage == 2:
                        sp.wait_ge(proj_out, past(c + 1))
                        sp.dma_start(projected[bass.ds(c * CH, CH), :].rearrange("(b p) f -> p b f", p=P),
                                     proj_sb[:, :].rearrange("p (b f) -> p b f", b=NB)).then_inc(proj_written, 16)
                chunks(sp, stage, body)

            for g in range(RING):
                layer0(Turn(0, g, G), True)
            groups(sp, RING, G, layer0)
            store(0)
            groups(sp, 0, G, layer1)
            store(1)
            sp.wait_ge(logit_written, past(16 * C))
            groups(sp, 0, G, layer2)
            store(2)
            sp.wait_ge(proj_written, past(16 * C))
            sp.wait_ge(stack_zero, 1)
            groups(sp, 0, G, layer3)

            for t in range(T):
                sp.wait_ge(scattered[t], 16 * G)

            def load_back(c):
                sp.wait_ge(back_mm, past(c))
                for t in range(T):
                    sp.dma_start(back_in[:, t, :, :], table_rows(back[t], c, 32)).then_inc(back_in_ld, 16)
                sp.wait_ge(x3_used, past(c))
                sp.dma_start(x3[:, :, :], table_rows(rows[3], c, 32)).then_inc(x3_in, 16)

            def store_out(c, size):
                sp.wait_ge(xn_ready, c + 3 * C + 1)
                full = size // P
                if full:
                    sp.dma_start(out[bass.ds(c * CH, full * P), :].rearrange("(b p) f -> p b f", p=P), xn[:, 0:full, 0:32])\
                      .then_inc(out_written, 16)
                if size % P:
                    left = size % P
                    sp.dma_start(out[bass.ds(c * CH + full * P, left), :], xn[0:left, full, 0:32]).then_inc(out_written, 16)

            whole = N // CH
            assert whole < C
            load_back(0)
            if whole:
                with sp.Fori(0, whole) as c:
                    load_back(c + 1)
                    store_out(c, CH)
            stores = whole
            for c in range(whole, C):
                if c + 1 < C:
                    load_back(c + 1)
                size = N - c * CH
                store_out(c, size)
                stores += (size >= P) + (size % P > 0)
            sp.wait_ge(out_written, past(16 * stores))

        @block.sync
        def _(sp):
            def c(dst, src, slow=False):
                CONSTS.append(1)
                sp.dma_start(dst, src, allow_slow_non_contiguous=slow).then_inc(const_in, 16)

            sp.wait_ge(zeroed, 1)
            per = (NT + P) * 32 // P
            assert per <= NT
            for t in range(T):
                sp.dma_start(back[t].rearrange("(p n) f -> p (n f)", p=P), S[:, 0:per]).then_inc(back_zero, 16)
            sp.wait_ge(const_ready, 1)
            c(ident[:, :], a["c_ident"])
            c(iota[:, :], a["c_iota"])
            c(tri[:, :], a["c_tri"])
            c(pcol[:, :], a["c_pcol"])
            c(fold0[:, :], a["c_fold0"])
            c(fold1[:, :], a["c_fold1"])
            c(wsel_r[:, :, :], a["c_wsel_r"])
            c(wsel_c[:, :, :], a["c_wsel_c"])
            for k in range(2):
                c(w1[32 * k:32 * k + 32, 64 * k:64 * k + 64], a["L0_gnn_W1"])
                c(b1[64 * k:64 * k + 64, :], a["L0_gnn_b1"])
            for to, frm in enumerate((0, 3, 1, 2)):
                c(w2[0:64, to * 64:to * 64 + 64], a["L0_gnn_W2"][:, frm * 64:frm * 64 + 64])
                c(w2[64:65, to * 64:to * 64 + 64], a["L0_gnn_b2"][:, frm * 64:frm * 64 + 64])
            c(si[64:72, 0:8], a["L0_gnn_si_w0"])
            for m in range(3):
                c(si[72 + m:96:3, 8 + m:32:3], a["L0_gnn_si_w1"], True)
            c(wall[:, :], a["L1_gnn_W"].rearrange("c i o -> (c i) o"))
            c(att[:, 0:32], a["L2_gnn_w2_W"])
            c(att[:, 32:33], a["L2_gnn_w2_b"].rearrange("a o -> o a"))
            c(a_col[:, :], a["L2_gnn_a"].rearrange("a o -> o a"))
            c(lin2[64:96, :], a["w1_WT"])
            c(lin2[96:97, :], a["L2_gnn_w1_b"])
            c(lin2[0:32, :], a["w2_WT"])
            c(lin2[32:33, :], a["L2_gnn_w2_b"])
            c(proj[64:96, 0:64], a["L3_gnn_W1f"][0:32, :])
            c(proj[64:96, 64:128], a["L3_gnn_W1b"][32:64, :])
            c(rest3[0:32, 0:64], a["L3_gnn_W1f"][32:64, :])
            c(rest3[0:32, 64:128], a["L3_gnn_W1b"][0:32, :])
            c(rest3[32:48, 0:64], a["L3_gnn_W1f"][64:80, :])
            c(rest3[32:48, 64:128], a["L3_gnn_W1b"][64:80, :])
            c(b13[0:64, :], a["L3_gnn_b1f"])
            c(b13[64:128, :], a["L3_gnn_b1b"])
            c(w23[0:64, 0:32], a["L3_gnn_W2f"])
            c(w23[64:128, 32:64], a["L3_gnn_W2b"])
            c(b23[:, 0:32], a["L3_gnn_b2f"])
            c(b23[:, 32:64], a["L3_gnn_b2b"])
            c(w1n[:, :], a["L3_gnn_W1n"])
            c(b1n[:, :], a["L3_gnn_b1n"])
            c(w2n[0:64, :], a["L3_gnn_W2n"])
            c(w2n[64:65, :], a["L3_gnn_b2n"])
            sp.dma_start(dst_all[:, :], a["dst_pg"]).then_inc(prep_in, 16)
            for k in range(GA):
                if k:
                    sp.wait_ge(prep_min, k)
                if GP <= W:
                    view = span_in[0:GP, :]
                else:
                    view = junk[0:GP, :].bitcast(I32)
                sp.dma_start(view, a["dst"].rearrange("(p k e) -> k p e", p=GP, e=E)[k, :, :]).then_inc(prep_in, 16)
            sp.wait_ge(prep_min, GA + 1)
            sp.dma_start(base_d.rearrange("(p k) -> p k", p=GP), gmin[0:GP, 0, :]).then_inc(prep_out, 16)
            sp.dma_start(span_d.rearrange("(p k) -> p k", p=GP), gmin[0:GP, 2, :]).then_inc(prep_out, 16)
            sp.wait_ge(prep_out, 32)
            sp.dma_start(base_f[:, :], base_d.rearrange("(o g) -> o g", o=1).to_broadcast([P, G])).then_inc(prep_back, 16)
            sp.dma_start(junk[0:1, 0:G], span_d.rearrange("(o g) -> o g", o=1)).then_inc(prep_back, 16)
            sp.wait_ge(back_zero, 16 * T)
            sp.dma_start(S[64:96, :], a["xT"]).then_inc(xT_in, 16)
            sp.wait_ge(flag_ready, 1)
            is_wide = sp.value_load(narrow_i[0:1, 0:1], min_val=0, max_val=1)
            with sp.If(is_wide == 0):
                sp_program(sp, False)
            with sp.Else():
                sp_program(sp, True)

        def pool_program(pool, wide):
            def gather(layer):
                def body(turn):
                    slot, lap, _ = turn.ring(layer)
                    pool.wait_ge(idx_loaded[slot], lap * 16 + 16)
                    pool.wait_ge(slot_free[slot], past(lap))
                    standing(pool)
                    w = WIDTH[layer]
                    for t in range(T):
                        pool.indirect_dma_start(xs[:, slot, t * w:(t + 1) * w], None, rows[layer][:, :],
                                                bass.IndirectOffsetOnAxis(ap=idx[:, slot, t:t + 1], axis=0))\
                            .then_inc(gathered[slot], 16)
                return body

            def scatter(turn, first=False):
                for t in () if first else range(T):
                    pool.wait_ge(scattered[t], turn.g * 16)
                pool.wait_ge(index_ready, turn.g + 1)
                wait_used(pool, turn, 3)
                pool.sem_inc(retired, 1)
                slot = turn.ring(3)[0]
                for t in range(T):
                    pool.indirect_dma_start(back[t][:, :], bass.IndirectOffsetOnAxis(ap=back_idx[:, slot, t:t + 1], axis=0),
                                            comb[:, slot, t * 32:(t + 1) * 32], None, compute_op=ALU.add)\
                        .then_inc(scattered[t], 16)

            if wide:
                groups(pool, 0, G, gather(0))
            else:
                behind = RING + 1

                def add0(turn):
                    node = pool.value_load(base_i[0:1, bass.ds(turn.g, 1)], min_val=0, max_val=N - 1)
                    pool.wait_ge(sums_out, past(turn.g + 1))
                    pool.wait_ge(added[0], past(turn.g))
                    standing(pool)
                    win = S[0:56, bass.ds(node, W)]
                    pool.tensor_tensor(win, sums0[:, turn.c % RING, :], win, ALU.add).then_inc(added[0], 1)

                def gather_and_add(turn):
                    gather(0)(turn)
                    add0(turn.near(-behind))
                for g in range(behind):
                    gather(0)(Turn(0, g, G))
                groups(pool, behind, G, gather_and_add)
                for g in range(G - behind, G):
                    add0(Turn(0, g, G))
            for layer in (1, 2):
                pool.wait_ge(table_written, past(16 * C * layer))
                groups(pool, 0, G, gather(layer))
            pool.wait_ge(table_written, past(16 * C * 3))
            pool.wait_ge(back_zero, 16 * T)
            pool.sem_inc(retired, RING - 2)
            lead = 3
            for g in range(lead):
                gather(3)(Turn(0, g, G))

            def both(turn, first=False):
                gather(3)(turn.near(lead))
                scatter(turn, first)
            both(Turn(0, 0, G), True)
            groups(pool, 1, G - lead, both)
            for g in range(G - lead, G):
                scatter(Turn(0, g, G))

        @block.gpsimd
        def _(pool):
            pool.memset(S[:, :], 0.0).then_inc(zeroed, 1)
            pool.wait_ge(flag_ready, 1)
            is_wide = pool.value_load(narrow_i[0:1, 0:1], min_val=0, max_val=1)
            with pool.If(is_wide == 0):
                pool_program(pool, False)
            with pool.Else():
                pool_program(pool, True)

        def pe_program(pe, wide):
            hid_ps = [bank(0, HALF), bank(1, HALF)]
            w_ps = ps[:, 2 * 512:5 * 512]
            agg0_ps = [bank(5)[0:56, 0:W], bank(6)[0:56, 0:W]]

            def hidden0(turn):
                slot, _, local = turn.ring(0)
                pe.wait_ge(attrs[0][slot], local * 48 + 48)
                pe.wait_ge(hid_act, past(turn.g * 2))
                pe.matmul(hid_ps[turn.c % 2], w1[:, :], featT[0:64, slot, :], start=True, stop=True).then_inc(hid_mm, 1)

            def weights0(turn, first=False):
                for j, tiles in enumerate(((0, 1), (2, 3), (4,))):
                    pe.wait_ge(hid_act, past(turn.g * 2 + (1 if j == 0 else 2)))
                    if not first:
                        pe.wait_ge(prods, turn.g * 3 + (j - 2))
                    for t in tiles:
                        last = pe.matmul(w_ps[:, t * 256:(t + 1) * 256], hidT[0:65, turn.c % 2, t * P:(t + 1) * P],
                                         w2[:, :], start=True, stop=True)
                    last.then_inc(w_mm, 1)

            def agg0(turn, s, slot, oh, bank_free):
                wait_used(pe, turn, 0)
                pe.wait_ge(onehot_ready[0], s + 1)
                if wide:
                    pe.wait_ge(added[0], past(s))
                elif bank_free is not None:
                    pe.wait_ge(sums_out, past(bank_free))
                for t in range(T):
                    last = pe.matmul(agg0_ps[oh], msg0[:, slot, t, :], onehot[:, oh, t, :], start=(t == 0), stop=(t == T - 1))
                last.then_inc(agg_mm[0], 1)

            if not wide:
                t0 = Turn(0, 0, G)
                hidden0(t0)
                hidden0(t0.near(1))
                weights0(t0, True)

                def agg_before(turn, first=False):
                    p = turn.near(-1)
                    agg0(p, p.g, p.c % 2, p.c % 2, None if first else p.g - 1)

                def body(turn, first=False):
                    hidden0(turn.near(1))
                    weights0(turn)
                    agg_before(turn, first)
                body(t0.near(1), True)
                groups(pe, 2, G - 1, body)
                last = Turn(0, G - 1, G)
                weights0(last)
                agg_before(last)
                agg_before(last.near(1))
            else:
                def body(turn, first=False):
                    hidden0(turn)
                    weights0(turn, first)
                    windows(pe, turn, lambda s, node: agg0(turn, s, turn.c % 2, 0, None))
                body(Turn(0, 0, G), True)
                groups(pe, 1, G, body)

            y_ps = bank(7)[:, 0:NB * 32]
            xt_ps = ps[:, 4 * 512:4 * 512 + CH]

            def to_features(n):
                pe.wait_ge(xn_ready, n + 1)
                pe.wait_ge(xt_copied, past(n))
                for b in range(NB):
                    last = pe.matmul(xt_ps[64:96, b * P:(b + 1) * P], xn[:, b, 0:32], ident[:, :], start=True, stop=True)
                last.then_inc(xt_mm, 1)

            def fold_nodes(stage, weights):
                def fold(n):
                    pe.wait_ge(chunk_copied, n + 1)
                    pe.wait_ge(centered, past(n))
                    for b in range(NB):
                        last = pe.matmul(y_ps[:, b * 32:(b + 1) * 32], chunk[0:96, b * P:(b + 1) * P], weights[:, :],
                                         start=True, stop=True)
                    last.then_inc(y_mm, 1)

                def body(c, n):
                    fold(n + 1)
                    to_features(n)
                fold(stage * C)
                chunks(pe, stage, body, C - 1)
                to_features(stage * C + C - 1)
            fold_nodes(0, fold0)

            agg1_ps = [bank(0)[:, 0:W], bank(1)[0:120, 0:W]]
            mix_ps = bank(2)[0:32, 0:W]

            def agg1(turn, s, slot, oh):
                wait_used(pe, turn, 1)
                pe.wait_ge(onehot_ready[1], s + 1)
                pe.wait_ge(agg_out, past(s))
                for k, (lo, hi) in enumerate(((0, 128), (128, 248))):
                    for t in range(T):
                        last = pe.matmul(agg1_ps[k], prod[:, slot, t, lo:hi], onehot[:, oh, t, :], start=(t == 0), stop=(t == T - 1))
                last.then_inc(agg_mm[1], 1)

            def mix1(s):
                pe.wait_ge(agg_out, past(s + 1))
                pe.wait_ge(added[1], past(s))
                pe.matmul(mix_ps, mix[:, 0, :], agg_sb[:, 0:W], start=True, stop=False)
                pe.matmul(mix_ps, mix[0:120, 1, :], agg_sb[0:120, W:2 * W], start=False, stop=True).then_inc(mix_mm, 1)

            if not wide:
                agg1(Turn(0, 0, G), 0, 0, 0)

                def body(turn):
                    mix1(turn.near(-1).g)
                    agg1(turn, turn.g, turn.c % 2, turn.c % 2)
                groups(pe, 1, G, body)
                mix1(G - 1)
            else:
                def body(turn):
                    def window(s, node):
                        agg1(turn, s, turn.c % 2, 0)
                        mix1(s)
                    windows(pe, turn, window)
                groups(pe, 0, G, body)
            fold_nodes(1, fold1)

            logit_ps = [ps[:, 0:2 * 512], ps[:, 6 * 512:8 * 512]]
            r_ps = bank(2)[:, 0:W]
            m_ps = [bank(3)[0:33, 0:W], bank(4)[0:33, 0:W]]
            att_ps = bank(5)[0:33, 0:W]

            def logits(turn, s, buf, free):
                slot, lap, _ = turn.ring(2)
                pe.wait_ge(gathered[slot], lap * (16 * T) + 16 * T)
                if free is not None:
                    pe.wait_ge(max_ready, past(free))
                for t in range(T):
                    last = pe.matmul(logit_ps[buf][0:W, t * P:(t + 1) * P],
                                     xs[:, slot, t * 34 + 33:t * 34 + 34].to_broadcast([P, W]), ident[:, :], start=True, stop=True)
                last.then_inc(logit_mm, 1)

            def spread_max(s, mslot):
                pe.wait_ge(max_ready, past(s + 1))
                pe.matmul(r_ps, mcol[:, 2:3].to_broadcast([W, P]), ident[0:W, 0:W], start=True, stop=True)
                pe.matmul(m_ps[mslot], mcol[:, 1:2].to_broadcast([W, 33]), ident[0:W, 0:W], start=True, stop=True)\
                  .then_inc(bcast_mm, 1)

            def attend(s, oh):
                pe.wait_ge(onehot_ready[2], s + 1)
                pe.wait_ge(weighed, past(s + 1))
                pe.wait_ge(added[2], past(s))
                for t in range(T):
                    last = pe.matmul(att_ps, val[:, t, :], onehot[:, oh, t, :], start=(t == 0), stop=(t == T - 1))
                last.then_inc(agg_mm[2], 1)

            if not wide:
                logits(Turn(0, 0, G), 0, 0, None)

                def body(turn):
                    spread_max(turn.g, turn.c % 2)
                    nxt = turn.near(1)
                    logits(nxt, nxt.g, nxt.c % 2, turn.g)
                    attend(turn.g, turn.c % 2)
                groups(pe, 0, G - 1, body)
                spread_max(G - 1, (G - 1) % 2)
                attend(G - 1, (G - 1) % 2)
            else:
                def body(turn):
                    def window(s, node):
                        logits(turn, s, 0, s)
                        spread_max(s, 0)
                        attend(s, 0)
                    windows(pe, turn, window)
                groups(pe, 0, G, body)

            mid_ps = ps[:, 512:512 + CH]

            def attention_nodes(c, n):
                pe.wait_ge(chunk_copied, n + 1)
                pe.wait_ge(hs_ready, past(c))
                for b in range(NB):
                    last = pe.matmul(bank(0)[:, b * 33:(b + 1) * 33], chunk[0:33, b * P:(b + 1) * P], ident[0:33, 0:33],
                                     start=True, stop=True)
                last.then_inc(tr_mm, 1)
                pe.wait_ge(hs_ready, past(c + 1))
                pe.wait_ge(proj_out, past(c))
                for b in range(NB):
                    last = pe.matmul(mid_ps[0:33, b * P:(b + 1) * P], hs[:, b, :], ident[:, :], start=True, stop=True)
                last.then_inc(hs_mm, 1)
                pe.wait_ge(hs_out, c + 1)
                pe.wait_ge(centered, past(n))
                for b in range(NB):
                    last = pe.matmul(y_ps[:, b * 32:(b + 1) * 32], chunk[0:97, b * P:(b + 1) * P], lin2[:, :],
                                     start=True, stop=True)
                last.then_inc(y_mm, 1)
                to_features(n)
                pe.wait_ge(xt_copied, past(n + 1))
                for b in range(NB):
                    last = pe.matmul(mid_ps[:, b * P:(b + 1) * P], xTs[64:96, b * P:(b + 1) * P], proj[64:96, :],
                                     start=True, stop=True)
                last.then_inc(proj_mm, 1)
            chunks(pe, 2, attention_nodes)

            srcT_ps = ps[:, 0:2 * 512]
            pre_ps = [bank(2, HALF), bank(3, HALF)]
            lin_ps = bank(4)[:, 0:T * 64]
            comb_ps = bank(5)[:, 0:T * 32]
            fwd_ps = bank(6)[0:32, 0:W]

            def srcT(turn):
                slot, lap, _ = turn.ring(3)
                pe.wait_ge(gathered[slot], lap * (16 * T) + 16 * T)
                pe.wait_ge(srcT_out, past(turn.g))
                for t in range(T):
                    last = pe.transpose(srcT_ps[0:32, t * P:(t + 1) * P], xs[:, slot, t * 32:(t + 1) * 32], ident[:, :])
                last.then_inc(srcT_mm, 1)

            def pre(turn):
                slot, lap, local = turn.ring(3)
                pe.wait_ge(srcT_out, past(turn.g + 1))
                pe.wait_ge(attrs[3][slot], local * 48 + 48)
                pe.wait_ge(stack_zero, 1)
                pe.wait_ge(pre_act, past(turn.g * 2))
                if not wide:
                    pe.wait_ge(onehotT_ready, turn.g + 1)
                    pe.wait_ge(win_loaded[1][slot], local * 16 + 16)
                if not wide:
                    for h in range(2):
                        pe.matmul(pre_ps[h], first3[:, slot, :], stack[:, slot, h * HALF:(h + 1) * HALF],
                                  start=True, stop=True).then_inc(pre_mm, 1)
                else:
                    for h in range(2):
                        last = pe.matmul(pre_ps[h], first3[:, 1, :], stack[:, slot, h * HALF:(h + 1) * HALF],
                                         start=True, stop=False)
                    last.then_inc(rest_mm, 1)

                    def window(s, node):
                        pe.wait_ge(onehotT_ready, s + 1)
                        pe.wait_ge(win_loaded[1][0], s * 16 + 16)
                        for h in range(2):
                            last = pe.matmul(pre_ps[h], first3[:, 0, :], stack[:, slot, h * HALF:(h + 1) * HALF],
                                             start=False, stop=False)
                        last.then_inc(win_mm, 1)
                    windows(pe, turn, window)
                    for h in range(2):
                        pe.matmul(pre_ps[h], ones[:, :], zrow[:, :], start=False, stop=True).then_inc(pre_mm, 1)

            def second(turn):
                pe.wait_ge(pre_act, past(turn.g * 2 + 2))
                pe.wait_ge(msg3_ready, past(turn.g))
                for t in range(T):
                    pe.matmul(lin_ps[:, t * 64:(t + 1) * 64], hidden3[:, t * P:(t + 1) * P], w23[:, :], start=True, stop=False)
                    last = pe.matmul(lin_ps[:, t * 64:(t + 1) * 64], ones[:, :], b23[:, :], start=False, stop=True)
                last.then_inc(lin_mm, 1)

            def fwd_agg(turn, s):
                pe.wait_ge(onehot_ready[3], s + 1)
                pe.wait_ge(added[3], past(s))
                for t in range(T):
                    last = pe.matmul(fwd_ps, msg3[:, t, 0:32], onehot[:, 0, t, :], start=(t == 0), stop=(t == T - 1))
                last.then_inc(agg_mm[3], 1)

            def combine(turn):
                pe.wait_ge(msg3_ready, past(turn.g + 1))
                wait_used(pe, turn.near(-1), 3)
                standing(pe)
                if not wide:
                    fwd_agg(turn, turn.g)
                else:
                    windows(pe, turn, lambda s, node: fwd_agg(turn, s))
                pe.wait_ge(same_ready, turn.g + 1)
                for t in range(T):
                    last = pe.matmul(comb_ps[:, t * 32:(t + 1) * 32], same[:, t, :], msg3[:, t, 32:64], start=True, stop=True)
                last.then_inc(comb_mm, 1)

            t0 = Turn(0, 0, G)
            srcT(t0)

            def body(turn):
                pre(turn)
                srcT(turn.near(1))
                second(turn)
                combine(turn)
            groups(pe, 0, G - 1, body)
            last = Turn(0, G - 1, G)
            pre(last)
            second(last)
            combine(last)

            def flow_nodes(c, n):
                pe.wait_ge(back_in_ld, c * (16 * T) + 16 * T)
                pe.wait_ge(flow_ready, past(c))
                for b in range(NB):
                    for t in range(T):
                        last = pe.matmul(mid_ps[32:64, b * P:(b + 1) * P], back_in[:, t, b, :], ident[:, :],
                                         start=(t == 0), stop=(t == T - 1))
                last.then_inc(back_mm, 1)
                pe.wait_ge(flow_ready, past(c + 1))
                pe.wait_ge(nh_ready, past(c))
                standing(pe)
                for lo in range(0, CH, 512):
                    hi = min(lo + 512, CH)
                    last = pe.matmul(xt_ps[0:64, lo:hi], w1n[:, :], flow[:, lo:hi], start=True, stop=True)
                last.then_inc(nh_mm, 1)
                pe.wait_ge(nh_ready, past(c + 1))
                pe.wait_ge(centered, past(n))
                for b in range(NB):
                    last = pe.matmul(y_ps[:, b * 32:(b + 1) * 32], nh[:, b * P:(b + 1) * P], w2n[:, :], start=True, stop=True)
                last.then_inc(y_mm, 1)
            chunks(pe, 3, flow_nodes)

        @block.tensor
        def _(pe):
            for c in counting:
                pe.sem_inc(c, 1)
            pe.wait_ge(const_in, 16 * len(CONSTS))
            pe.wait_ge(const_ready, 2)
            for k in range(4):
                last = pe.matmul(bank(0)[:, k * 8:k * 8 + 8], wsel_r[:, k, :], wall[:, :], start=True, stop=True)
            pe.matmul(bank(1)[:, 0:33], a_col[:, 0:1].to_broadcast([32, P]), att[:, :], start=True, stop=True)\
              .then_inc(weights_mm, 1)
            pe.wait_ge(const_ready, 3)
            pe.wait_ge(flag_ready, 1)
            is_wide = pe.value_load(narrow_i[0:1, 0:1], min_val=0, max_val=1)
            with pe.If(is_wide == 0):
                pe_program(pe, False)
            with pe.Else():
                pe_program(pe, True)

        def act_program(act, wide):
            mid_ps = ps[:, 512:512 + CH]
            xt_ps = ps[:, 4 * 512:4 * 512 + CH]

            def relu0(turn):
                act.wait_ge(hid_mm, turn.g + 1)
                hid = bank(turn.c % 2, HALF)
                act.activation(hidT[0:64, turn.c % 2, 0:HALF], hid[0:64, :], ACT.Relu, bias=b1[0:64, :]).then_inc(hid_act, 1)
                act.activation(hidT[0:64, turn.c % 2, HALF:E], hid[64:128, 0:HALF], ACT.Relu, bias=b1[64:128, :])\
                   .then_inc(hid_act, 1)

            def sums(turn, first=False):
                act.wait_ge(agg_mm[0], past(turn.g + 1))
                if not first:
                    act.wait_ge(added[0], past(turn.g - RING + 1))
                standing(act)
                act.activation(sums0[:, turn.c % RING, :], bank(5 + turn.c % 2)[0:56, 0:W], ACT.Copy).then_inc(sums_out, 1)

            def scale0(turn, first=False):
                slot, lap, local = turn.ring(0)
                act.wait_ge(gathered[slot], lap * (16 * T) + 16 * T)
                act.wait_ge(attrs[0][slot], local * 48 + 48)
                if not first:
                    act.wait_ge(prods, turn.g * 3 - 3)
                standing(act)
                for t in range(T):
                    last = act.activation(vs[:, turn.c % 2, t, :].rearrange("p (m i) -> p m i", m=3),
                                          xs[:, slot, t * 32 + 8:(t + 1) * 32].rearrange("p (i m) -> p m i", m=3), ACT.Copy,
                                          scale=sh[:, slot, 4 * t:4 * t + 1])
                last.then_inc(scaled, 1)

            def onehot0(turn):
                act.drain()
                for t in range(T):
                    act.activation(apart[:, t, :], iota[:, :], ACT.Square, bias=rel[:, bass.ds(turn.g * T + t, 1)], scale=-1.0)
                act.drain()
                act.activation(onehot[:, turn.c % 2, :, :], apart[:, :, :], ACT.Relu, bias=unit[:, :], scale=-1.0)\
                   .then_inc(onehot_ready[0], 1)

            if wide:
                groups(act, 0, G, relu0)
            else:
                def body(turn, first=False):
                    relu0(turn)
                    scale0(turn)
                    sums(turn.near(-2), first)
                    onehot0(turn)
                act.wait_ge(rel_ready, 1)
                for g in range(2):
                    relu0(Turn(0, g, G))
                    scale0(Turn(0, g, G), True)
                    onehot0(Turn(0, g, G))
                for g in range(2, RING + 2):
                    body(Turn(0, g, G), True)
                groups(act, RING + 2, G, body)
                for g in range(G - 2, G):
                    sums(Turn(0, g, G))

            def copy_chunk(c, n):
                act.wait_ge(y_mm, past(n))
                act.activation(chunk[0:96, :], S[0:96, bass.ds(c * CH, CH)], ACT.Copy).then_inc(chunk_copied, 1)

            def std(n):
                act.wait_ge(var_ready, n + 1)
                act.activation(stat[:, 2, :], stat[:, 1, :], ACT.Sqrt, bias=eps[:, :], scale=1.0 / 32).then_inc(std_ready, 1)

            def features(c, n, extra=False):
                act.wait_ge(xt_mm, past(n + 1))
                if extra:
                    act.wait_ge(proj_mm, past(c))
                    act.activation(xTs[64:96, :], xt_ps[64:96, :], ACT.Copy)
                act.activation(S[64:96, bass.ds(c * CH, CH)], xt_ps[64:96, :], ACT.Copy).then_inc(xt_copied, 1)

            def simple(layer):
                def body(c, n):
                    copy_chunk(c + 1, n + 1)
                    std(n)
                    features(c, n)
                act.wait_ge(added[layer], past(steps(wide)))
                last = layer * C + C - 1
                copy_chunk(0, layer * C)
                chunks(act, layer, body, C - 1)
                std(last)
                features(C - 1, last)
            act.wait_ge(xT_in, 16)
            simple(0)

            def out1(s):
                act.wait_ge(agg_mm[1], past(s + 1))
                act.wait_ge(mix_mm, past(s))
                act.activation(agg_sb[:, 0:W], bank(0)[:, 0:W], ACT.Copy)
                act.activation(agg_sb[0:120, W:2 * W], bank(1)[0:120, 0:W], ACT.Copy).then_inc(agg_out, 1)

            def body(turn):
                if not wide:
                    out1(turn.g)
                else:
                    windows(act, turn, lambda s, node: out1(s))
            groups(act, 0, G, body)
            simple(1)

            def exp_edges(s):
                act.wait_ge(expo_ready, s + 1)
                act.wait_ge(weighed, past(s))
                act.activation(aexp[:, :], expo[:, 1, :], ACT.Exp).then_inc(exp_done, 1)

            def exp_scales(s):
                act.wait_ge(diff_ready, s + 1)
                act.activation(merge[:, 3:5, :], merge[:, 1:3, :], ACT.Exp).then_inc(scale_done, 1)

            def penalty(turn, first=False):
                slot, _, local = turn.ring(2)
                act.wait_ge(attrs[2][slot], local * 16 + 16)
                if not first:
                    act.wait_ge(max_ready, past(turn.g))
                standing(act)
                act.activation(pen[:, :], dst_row[0:W, slot, :], ACT.Square, bias=node_steep[:, bass.ds(turn.g, 1)], scale=-STEEP)\
                   .then_inc(pen_ready, 1)

            if not wide:
                t0 = Turn(0, 0, G)
                penalty(t0, True)
                penalty(t0.near(1))
                exp_edges(0)

                def body(turn, last=False):
                    exp_scales(turn.near(-1).g)
                    if not last:
                        penalty(turn.near(1))
                    exp_edges(turn.g)
                groups(act, 1, G - 1, body)
                body(Turn(0, G - 1, G), True)
                exp_scales(G - 1)
            else:
                def body(turn):
                    def window(s, node):
                        exp_edges(s)
                        exp_scales(s)
                    windows(act, turn, window)
                groups(act, 0, G, body)

            def attention_nodes(c, n):
                copy_chunk(c, n)
                act.wait_ge(hs_mm, past(c + 1))
                act.activation(chunk[0:33, :], mid_ps[0:33, :], ACT.Copy).then_inc(hs_out, 1)
                std(n)
                features(c, n, True)
                act.wait_ge(proj_mm, past(c + 1))
                act.wait_ge(proj_written, past(c * 16))
                act.activation(proj_sb[:, :], mid_ps, ACT.Copy).then_inc(proj_out, 1)
            act.wait_ge(added[2], past(steps(wide)))
            chunks(act, 2, attention_nodes)

            def srcT(turn):
                slot, lap, _ = turn.ring(3)
                act.wait_ge(srcT_mm, turn.g + 1)
                act.wait_ge(slot_free[slot], past(lap))
                act.activation(stack[0:32, slot, :], ps[0:32, 0:E], ACT.Copy).then_inc(srcT_out, 1)

            def relu3(turn):
                act.wait_ge(lin_mm, past(turn.g))
                for h in range(2):
                    act.wait_ge(pre_mm, turn.g * 2 + h + 1)
                    act.activation(hidden3[:, h * HALF:(h + 1) * HALF], bank(2 + h, HALF), ACT.Relu, bias=b13[:, :])\
                       .then_inc(pre_act, 1)

            def relu_out(turn):
                act.wait_ge(lin_mm, past(turn.g + 1))
                act.wait_ge(comb_mm, past(turn.g))
                act.activation(msg3[:, :, :], bank(4)[:, 0:T * 64], ACT.Relu).then_inc(msg3_ready, 1)

            def comb_out(turn):
                act.wait_ge(comb_mm, past(turn.g + 1))
                act.wait_ge(index_ready, turn.g + 1)
                act.wait_ge(retired, past(turn.g))
                slot = turn.ring(3)[0]
                act.activation(comb[:, slot, :], bank(5)[:, 0:T * 32], ACT.Copy).then_inc(slot_free[slot], 1)

            act.wait_ge(stack_zero, 1)
            srcT(Turn(0, 0, G))

            def body(turn):
                relu3(turn)
                srcT(turn.near(1))
                relu_out(turn)
                comb_out(turn)
            groups(act, 0, G - 1, body)
            last = Turn(0, G - 1, G)
            relu3(last)
            relu_out(last)
            comb_out(last)

            def flow_nodes(c, n):
                act.wait_ge(back_mm, past(c + 1))
                act.wait_ge(nh_mm, past(c))
                act.activation(flow[0:32, :], S[0:32, bass.ds(c * CH, CH)], ACT.Copy)
                act.activation(flow[32:64, :], mid_ps[32:64, :], ACT.Copy).then_inc(flow_ready, 1)
                act.wait_ge(nh_mm, past(c + 1))
                act.wait_ge(y_mm, past(n))
                act.activation(nh[0:64, :], xt_ps[0:64, :], ACT.Relu, bias=b1n[:, :]).then_inc(nh_ready, 1)
                std(n)
            act.wait_ge(added[3], past(steps(wide)))
            chunks(act, 3, flow_nodes)

        @block.scalar
        def _(act):
            act.wait_ge(const_in, 16 * len(CONSTS))
            act.wait_ge(const_ready, 3)
            act.wait_ge(flag_ready, 1)
            is_wide = act.value_load(narrow_i[0:1, 0:1], min_val=0, max_val=1)
            with act.If(is_wide == 0):
                act_program(act, False)
            with act.Else():
                act_program(act, True)

        def dve_program(v, wide):
            def rel_of(turn):
                return rel[:, bass.ds(turn.g * T, T)]

            def one_hot(slot, r):
                return v.tensor_tensor(onehot[:, slot, :, :], iota[:, :].unsqueeze(1).to_broadcast([P, T, W]),
                                       r.unsqueeze(2).to_broadcast([P, T, W]), ALU.is_equal)

            def base_of(g):
                return v.value_load(base_i[0:1, bass.ds(g, 1)], min_val=0, max_val=N - 1)

            def add(layer, s, node, rows_, psum, done=None):
                v.wait_ge(agg_mm[layer] if done is None else done, past(s + 1))
                win = S[0:rows_, bass.ds(node, W)]
                v.tensor_tensor(win, psum, win, ALU.add).then_inc(added[layer], 1)
                v.drain()

            def wide_start(turn):
                v.tensor_copy(wrel[:, :], rel_of(turn))
                v.tensor_copy(wnode[:, :], pcol[:, 0:1])
                v.drain()

            def wide_next():
                v.drain()
                v.tensor_scalar(wrel[:, :], wrel[:, :], -float(W), None, ALU.add)
                v.tensor_scalar(wnode[:, :], wnode[:, :], float(W), None, ALU.add)
                v.drain()

            w_ps = ps[:, 2 * 512:5 * 512].rearrange("p (t f) -> p t f", f=256)

            def source0(turn):
                slot = turn.ring(0)[0]
                return xs[:, slot, 0:T * 32].rearrange("p (t f) -> p t f", t=T), sh[:, slot, 0:T * 4].rearrange("p (t f) -> p t f", t=T)

            def dot_terms(turn):
                slot, lap, local = turn.ring(0)
                v.wait_ge(gathered[slot], lap * (16 * T) + 16 * T)
                v.wait_ge(attrs[0][slot], local * 48 + 48)
                x, h = source0(turn)
                v.tensor_tensor(z[:, turn.c % 2, :, 0:8], x[:, :, 0:8], h[:, :, 0:1].to_broadcast([P, T, 8]), ALU.mult)
                v.tensor_tensor(vtmp[:, :, :, :], x[:, :, 8:32].rearrange("p t (i m) -> p t i m", m=3),
                                h[:, :, 1:4].unsqueeze(2).to_broadcast([P, T, 8, 3]), ALU.mult)

            def dots(turn):
                v.tensor_reduce(z[:, turn.c % 2, :, 8:16], vtmp[:, :, :, :], AX.X, ALU.add)

            def products0(turn):
                x, _ = source0(turn)
                vec = vs[:, turn.c % 2, :, :].rearrange("p t (m i) -> p t m i", m=3)
                for j, (lo, hi) in enumerate(((0, 2), (2, 4), (4, 5))):
                    n = hi - lo
                    v.wait_ge(w_mm, turn.g * 3 + j + 1)
                    v.tensor_tensor(pA[:, lo:hi, :, :], w_ps[:, lo:hi, 0:128].rearrange("p t (i o) -> p t i o", o=8),
                                    z[:, turn.c % 2, lo:hi, :].unsqueeze(3).to_broadcast([P, n, 16, 8]), ALU.mult)
                    v.tensor_tensor(pB[:, lo:hi, :, :], w_ps[:, lo:hi, 128:192].rearrange("p t (i o) -> p t i o", o=8),
                                    x[:, lo:hi, 0:8].unsqueeze(3).to_broadcast([P, n, 8, 8]), ALU.mult)
                    v.tensor_tensor(pC[:, lo:hi, :, :, :],
                                    w_ps[:, lo:hi, 192:256].rearrange("p t (i o) -> p t i o", o=8).unsqueeze(2)
                                    .to_broadcast([P, n, 3, 8, 8]),
                                    vec[:, lo:hi, :, :].unsqueeze(4).to_broadcast([P, n, 3, 8, 8]), ALU.mult)\
                     .then_inc(prods, 1)

            def channel_sums(turn):
                msg = msg0[:, turn.c % 2, :, :]
                v.tensor_reduce(msg[:, :, 0:8], pA[:, :, :, :].rearrange("p t i o -> p t o i"), AX.X, ALU.add)
                v.tensor_reduce(mB[:, :, :], pB[:, :, :, :].rearrange("p t i o -> p t o i"), AX.X, ALU.add)
                v.tensor_reduce(msg[:, :, 32:56].rearrange("p t (m o) -> p t m o", m=3),
                                pC[:, :, :, :, :].rearrange("p t m i o -> p t m o i"), AX.X, ALU.add)

            def outer0(turn):
                v.tensor_tensor(msg0[:, turn.c % 2, :, 8:32].rearrange("p t (o m) -> p t o m", m=3),
                                mB[:, :, :].unsqueeze(3).to_broadcast([P, T, 8, 3]),
                                source0(turn)[1][:, :, 1:4].unsqueeze(2).to_broadcast([P, T, 8, 3]), ALU.mult)\
                 .then_inc(slot_free[turn.ring(0)[0]], 1)

            agg0_ps = bank(5)[0:56, 0:W]

            def narrow_onehot(layer, turn, first=False):
                if not first:
                    v.wait_ge(agg_mm[layer], past(turn.g - 1))
                one_hot(turn.c % 2, rel_of(turn)).then_inc(onehot_ready[layer], 1)

            if not wide:
                def step(turn, first=False, last=False):
                    v.wait_ge(scaled, turn.g + 1)
                    products0(turn)
                    if not last:
                        dot_terms(turn.near(1))
                    v.drain()
                    if not first:
                        v.wait_ge(agg_mm[0], past(turn.g - 1))
                    channel_sums(turn)
                    if not last:
                        dots(turn.near(1))
                    v.drain()
                    outer0(turn)
                dot_terms(Turn(0, 0, G))
                v.drain()
                dots(Turn(0, 0, G))
                v.drain()
                step(Turn(0, 0, G), first=True)
                groups(v, 1, G - 1, step)
                step(Turn(0, G - 1, G), last=True)
            else:
                def body(turn):
                    dot_terms(turn)
                    x, h = source0(turn)
                    v.tensor_tensor(vs[:, turn.c % 2, :, :].rearrange("p t (m i) -> p t m i", m=3),
                                    x[:, :, 8:32].rearrange("p t (i m) -> p t m i", m=3),
                                    h[:, :, 0:1].unsqueeze(3).to_broadcast([P, T, 3, 8]), ALU.mult)
                    v.drain()
                    dots(turn)
                    v.drain()
                    products0(turn)
                    v.drain()
                    v.wait_ge(agg_mm[0], past(turn.g * NW))
                    channel_sums(turn)
                    v.drain()
                    outer0(turn)
                    wide_start(turn)

                    def window(s, node):
                        one_hot(0, wrel[:, :]).then_inc(onehot_ready[0], 1)
                        add(0, s, node, 56, agg0_ps)
                        wide_next()
                    windows(v, turn, window)
                groups(v, 0, G, body)

            y_ps = bank(7)[:, 0:NB * 32].rearrange("p (b f) -> p b f", b=NB)

            def clear(c):
                v.tensor_scalar(S[0:64, bass.ds(c * CH, CH)], zeros[:, :].to_broadcast([64, CH]), 0.0, None, ALU.add)

            def layer_norm(c, n, y):
                v.tensor_reduce(stat[:, 0, :], y, AX.X, ALU.add)
                v.drain()
                v.tensor_scalar(stat[:, 3, :], stat[:, 0, :], -1.0 / 32, None, ALU.mult)
                v.drain()
                v.tensor_tensor(yc[:, :, :], y, stat[:, 3, :].unsqueeze(2).to_broadcast([P, NB, 32]), ALU.add).then_inc(centered, 1)
                v.drain()
                v.tensor_tensor(sq[:, :, :], yc[:, :, :], yc[:, :, :], ALU.mult)
                v.drain()
                v.tensor_reduce(stat[:, 1, :], sq[:, :, :], AX.X, ALU.add).then_inc(var_ready, 1)
                if c is not None:
                    clear(c)
                v.wait_ge(std_ready, n + 1)
                v.reciprocal(stat[:, 4, :], stat[:, 2, :])
                v.drain()

            def normalized():
                return v.tensor_tensor(xn[:, :, 0:32], yc[:, :, :], stat[:, 4, :].unsqueeze(2).to_broadcast([P, NB, 32]), ALU.mult)

            def free_xn(c, n):
                v.wait_ge(table_written, past(n * 16))
                v.wait_ge(xt_mm, past(n))

            def plain_nodes(c, n):
                v.wait_ge(y_mm, past(n + 1))
                layer_norm(c, n, y_ps)
                free_xn(c, n)
                normalized().then_inc(xn_ready, 1)
                v.drain()
            chunks(v, 0, plain_nodes)

            def products1(turn, first=False):
                slot, lap, local = turn.ring(1)
                v.wait_ge(gathered[slot], lap * (16 * T) + 16 * T)
                v.wait_ge(attrs[1][slot], local * 48 + 48)
                if wide:
                    v.wait_ge(agg_mm[1], past(turn.g * NW))
                elif not first:
                    v.wait_ge(agg_mm[1], past(turn.g - 1))
                x = xs[:, slot, 0:T * 32].rearrange("p (t f) -> p t f", t=T)
                pr = prod[:, turn.c % 2, :, :]
                v.tensor_tensor(pr[:, :, 0:32], x, sh[:, slot, 0:T].unsqueeze(2).to_broadcast([P, T, 32]), ALU.mult)
                v.tensor_tensor(pr[:, :, 32:128].rearrange("p t (k f) -> p t k f", k=3), x.unsqueeze(2).to_broadcast([P, T, 3, 32]),
                                sh[:, slot, T:4 * T].rearrange("p (t k) -> p t k", t=T).unsqueeze(3).to_broadcast([P, T, 3, 32]),
                                ALU.mult)
                last = v.tensor_tensor(pr[:, :, 128:248].rearrange("p t (k f) -> p t k f", k=5),
                                       x[:, :, 8:32].unsqueeze(2).to_broadcast([P, T, 5, 24]),
                                       sh[:, slot, 4 * T:9 * T].rearrange("p (t k) -> p t k", t=T).unsqueeze(3)
                                       .to_broadcast([P, T, 5, 24]), ALU.mult)
                last.then_inc(slot_free[slot], 1)

            mix_ps = bank(2)[0:32, 0:W]
            if not wide:
                narrow_onehot(1, Turn(0, 0, G), True)
                products1(Turn(0, 0, G), True)

                def body(turn):
                    narrow_onehot(1, turn)
                    products1(turn)
                    p = turn.near(-1).g
                    add(1, p, base_of(p), 32, mix_ps, mix_mm)
                groups(v, 1, G, body)
                add(1, G - 1, base_of(G - 1), 32, mix_ps, mix_mm)
            else:
                def body(turn):
                    products1(turn)
                    wide_start(turn)

                    def window(s, node):
                        one_hot(0, wrel[:, :]).then_inc(onehot_ready[1], 1)
                        add(1, s, node, 32, mix_ps, mix_mm)
                        wide_next()
                    windows(v, turn, window)
                groups(v, 0, G, body)

            def attention_input(c, n):
                v.wait_ge(y_mm, past(n + 1))
                layer_norm(c, n, y_ps)
                free_xn(c, n)
                v.wait_ge(logit_written, past(c * 16))
                normalized()
                v.drain()
                v.tensor_tensor(sq[:, :, :], xn[:, :, 0:32], nu[:, 0:32].unsqueeze(1).to_broadcast([P, NB, 32]), ALU.mult)
                v.drain()
                v.tensor_reduce(xn[:, :, 33:34], sq[:, :, :], AX.X, ALU.add)
                v.drain()
                v.tensor_scalar(stat[:, 5, :].unsqueeze(2), xn[:, :, 33:34], -1.0, nu[:, 32:33], ALU.mult, ALU.add).then_inc(xn_ready, 1)
                v.drain()
            chunks(v, 1, attention_input)

            v.memset(M, -BIG)
            v.drain()
            logit_ps = [ps[0:W, 0:E], ps[0:W, 6 * 512:6 * 512 + E]]
            r_ps = bank(2)[:, 0:W]
            m_ps = [bank(3)[0:33, 0:W], bank(4)[0:33, 0:W]]
            att_ps = bank(5)[0:33, 0:W]

            def penalty(turn, node_col):
                slot, _, local = turn.ring(2)
                v.wait_ge(attrs[2][slot], local * 16 + 16)
                v.tensor_scalar(pen[:, :], dst_row[0:W, slot, :], node_col, BIG, ALU.not_equal, ALU.mult)

            def local_max(s, buf):
                v.wait_ge(logit_mm, s + 1)
                standing(v)
                v.tensor_tensor_reduce(out=junk[0:W, :], in0=logit_ps[buf], in1=pen[:, :], scale=1.0, scalar=-BIG,
                                       op0=ALU.subtract, op1=ALU.max, accum_out=mcol[:, 0:1])

            def logit_max(qslot, qcount):
                v.wait_ge(win_loaded[0][qslot], qcount)
                v.tensor_tensor(mcol[:, 1:2], mcol[:, 0:1], qwin[:, qslot:qslot + 1], ALU.add)

            def less_max(qslot):
                v.tensor_tensor(mcol[:, 2:3], qwin[:, qslot:qslot + 1], mcol[:, 1:2], ALU.subtract).then_inc(max_ready, 1)

            def own_max(s, oh):
                v.wait_ge(bcast_mm, past(s + 1))
                v.tensor_tensor(oh_r[:, :, :], r_ps.unsqueeze(1).to_broadcast([P, T, W]), onehot[:, oh, :, :], ALU.mult)
                v.drain()
                v.tensor_reduce(expo[:, 0, :], oh_r[:, :, :], AX.X, ALU.add)
                v.drain()

            def logit_part(turn):
                slot, _, _ = turn.ring(2)
                return xs[:, slot, :].rearrange("p (t f) -> p t f", t=T)[:, :, 33:34]

            def weigh(turn, s):
                slot, _, _ = turn.ring(2)
                x = xs[:, slot, :].rearrange("p (t f) -> p t f", t=T)
                v.wait_ge(exp_done, past(s + 1))
                v.wait_ge(agg_mm[2], past(s))
                last = v.tensor_tensor(val[:, :, :], x[:, :, 0:33], aexp[:, :].unsqueeze(2).to_broadcast([P, T, 33]), ALU.mult)
                last.then_inc(weighed, 1)

            def new_max(mslot, node):
                v.tensor_tensor(merge[:, 0, :], m_ps[mslot], M[:, bass.ds(node, W)], ALU.max)

            def max_steps(mslot, node):
                v.tensor_tensor(merge[:, 1, :], M[:, bass.ds(node, W)], merge[:, 0, :], ALU.subtract)
                v.tensor_tensor(merge[:, 2, :], m_ps[mslot], merge[:, 0, :], ALU.subtract)

            def keep_max(node):
                v.tensor_copy(M[:, bass.ds(node, W)], merge[:, 0, :])

            def scaled_sums(s, node):
                v.wait_ge(scale_done, s + 1)
                v.wait_ge(agg_mm[2], past(s + 1))
                v.tensor_tensor(merge[:, 5, :], S[0:33, bass.ds(node, W)], merge[:, 3, :], ALU.mult)
                v.tensor_tensor(merge[:, 1, :], att_ps, merge[:, 4, :], ALU.mult)

            def merge_sums(node):
                v.tensor_tensor(S[0:33, bass.ds(node, W)], merge[:, 5, :], merge[:, 1, :], ALU.add).then_inc(added[2], 1)

            if not wide:
                def prepare(turn, first=False):
                    if not first:
                        v.wait_ge(agg_mm[2], past(turn.g - 1))
                    one_hot(turn.c % 2, rel_of(turn)).then_inc(onehot_ready[2], 1)

                def step(turn, first=False, last=False):
                    p = turn.near(-1)
                    slot, _, local = turn.ring(2)
                    if not first:
                        node = base_of(p.g)
                        weigh(p, p.g)
                    v.wait_ge(pen_ready, turn.g + 1)
                    local_max(turn.g, turn.c % 2)
                    if not first:
                        new_max(p.c % 2, node)
                        v.drain().then_inc(slot_free[p.ring(2)[0]], 1)
                    else:
                        v.drain()
                    logit_max(slot, local * 16 + 16)
                    if not first:
                        max_steps(p.c % 2, node)
                        v.drain().then_inc(diff_ready, 1)
                    else:
                        v.drain()
                    less_max(slot)
                    if not first:
                        keep_max(node)
                    if not last:
                        prepare(turn.near(1), first)
                    if not first:
                        scaled_sums(p.g, node)
                        v.drain()
                        merge_sums(node)
                    own_max(turn.g, turn.c % 2)
                    v.tensor_tensor(expo[:, 1, :].unsqueeze(2), expo[:, 0, :].unsqueeze(2), logit_part(turn), ALU.add)\
                     .then_inc(expo_ready, 1)

                prepare(Turn(0, 0, G), True)
                v.drain()
                step(Turn(0, 0, G), first=True)
                groups(v, 1, G - 1, step)
                step(Turn(0, G - 1, G), last=True)
                node = base_of(G - 1)
                weigh(Turn(0, G - 1, G), G - 1)
                new_max((G - 1) % 2, node)
                v.drain().then_inc(slot_free[Turn(0, G - 1, G).ring(2)[0]], 1)
                max_steps((G - 1) % 2, node)
                v.drain().then_inc(diff_ready, 1)
                keep_max(node)
                scaled_sums(G - 1, node)
                v.drain()
                merge_sums(node)
                v.drain()
            else:
                def body(turn):
                    wide_start(turn)

                    def window(s, node):
                        penalty(turn, wnode[0:W, :])
                        v.drain()
                        local_max(s, 0)
                        v.drain()
                        logit_max(0, s * 16 + 16)
                        v.drain()
                        less_max(0)
                        one_hot(0, wrel[:, :]).then_inc(onehot_ready[2], 1)
                        v.drain()
                        own_max(s, 0)
                        v.tensor_tensor(expo[:, 2, :].unsqueeze(2), expo[:, 0, :].unsqueeze(2), logit_part(turn), ALU.add)
                        v.drain()
                        v.tensor_scalar(expo[:, 1, :], expo[:, 2, :], 1.0, None, ALU.min).then_inc(expo_ready, 1)
                        weigh(turn, s)
                        new_max(0, node)
                        v.drain()
                        max_steps(0, node)
                        v.drain().then_inc(diff_ready, 1)
                        keep_max(node)
                        scaled_sums(s, node)
                        v.drain()
                        merge_sums(node)
                        wide_next()
                    windows(v, turn, window)
                    v.drain().then_inc(slot_free[turn.ring(2)[0]], 1)
                groups(v, 0, G, body)

            def attention_nodes(c, n):
                sums = bank(0)[:, 0:NB * 33].rearrange("p (b f) -> p b f", b=NB)
                v.wait_ge(tr_mm, c + 1)
                v.tensor_scalar(stat[:, 3, :].unsqueeze(2), sums[:, :, 32:33], 1.0e-30, None, ALU.max)
                v.drain()
                v.reciprocal(stat[:, 4, :], stat[:, 3, :])
                v.drain()
                v.wait_ge(hs_mm, past(c))
                v.tensor_tensor(hs[:, :, :], sums, stat[:, 4, :].unsqueeze(2).to_broadcast([P, NB, 33]), ALU.mult).then_inc(hs_ready, 1)
                v.drain()
                v.wait_ge(y_mm, past(n + 1))
                layer_norm(c, n, y_ps)
                free_xn(c, n)
                normalized().then_inc(xn_ready, 1)
                v.drain()
            chunks(v, 2, attention_nodes)

            v.memset(stack[:, :, :], 0.0)
            for slot in ((1,) if wide else range(RING)):
                v.tensor_copy(first3[0:64, slot, :], rest3[:, :])
            v.drain().then_inc(stack_zero, 1)

            def target_onehot(turn, s, node_col):
                slot, _, local = turn.ring(3)
                v.wait_ge(attrs[3][slot], local * 48 + 48)
                if wide:
                    v.wait_ge(rest_mm, turn.g + 1)
                    v.wait_ge(win_mm, past(s))
                v.tensor_scalar(stack[64:128, slot, :], dst_row[64:128, slot, :], node_col, None, ALU.is_equal)\
                 .then_inc(onehotT_ready, 1)

            def same_source(turn):
                slot, lap, _ = turn.ring(3)
                v.wait_ge(comb_mm, past(turn.g))
                v.wait_ge(idx_loaded[slot], lap * 16 + 16)
                v.tensor_tensor(same[:, :, :], src_row[:, slot, :].rearrange("p (t e) -> p t e", t=T),
                                idx[:, slot, :].unsqueeze(2).to_broadcast([P, T, P]), ALU.is_equal).then_inc(same_ready, 1)
                v.tensor_scalar(back_tmp[:, 1, :], idx[:, slot, :], -1.0, pcol[:, 1:2], ALU.mult, ALU.add)
                v.drain()
                for t in range(T):
                    v.tensor_tensor_reduce(out=junk[:, t * P:(t + 1) * P], in0=same[:, t, :], in1=tri[:, :], scale=1.0, scalar=0.0,
                                           op0=ALU.mult, op1=ALU.add, accum_out=back_tmp[:, 0, t:t + 1])
                v.drain()
                v.scalar_tensor_tensor(back_tmp[:, 2, :], back_tmp[:, 0, :], 0.5, back_tmp[:, 1, :], ALU.is_gt, ALU.mult)
                v.drain()
                v.wait_ge(retired, past(turn.g))
                v.tensor_tensor(back_idx[:, slot, :], back_tmp[:, 2, :], idx[:, slot, :], ALU.add).then_inc(index_ready, 1)

            fwd_ps = bank(6)[0:32, 0:W]

            def onehot3(turn):
                v.wait_ge(agg_mm[3], past(turn.g))
                one_hot(0, rel_of(turn)).then_inc(onehot_ready[3], 1)
                v.drain()

            if not wide:
                def front3(turn):
                    target_onehot(turn, turn.g, node_of[64:128, bass.ds(turn.g, 1)])
                    same_source(turn)
                    onehot3(turn)
                front3(Turn(0, 0, G))

                def body(turn):
                    front3(turn)
                    p = turn.near(-1).g
                    add(3, p, base_of(p), 32, fwd_ps)
                groups(v, 1, G, body)
                add(3, G - 1, base_of(G - 1), 32, fwd_ps)
            else:
                def body(turn):
                    wide_start(turn)

                    def window(s, node):
                        target_onehot(turn, s, wnode[64:128, :])
                        wide_next()
                    windows(v, turn, window)
                    same_source(turn)
                    wide_start(turn)

                    def window(s, node):
                        v.wait_ge(agg_mm[3], past(s))
                        one_hot(0, wrel[:, :]).then_inc(onehot_ready[3], 1)
                        add(3, s, node, 32, fwd_ps)
                        wide_next()
                    windows(v, turn, window)
                groups(v, 0, G, body)

            def flow_nodes(c, n):
                v.wait_ge(y_mm, past(n + 1))
                v.wait_ge(x3_in, c * 16 + 16)
                v.scalar_tensor_tensor(sq[:, :, :], y_ps, 0.0, x3[:, :, :], ALU.max, ALU.add).then_inc(x3_used, 1)
                v.drain()
                layer_norm(None, n, sq[:, :, :])
            whole = N // CH

            def finish(c, stored):
                flow_nodes(c, c + 3 * C)
                v.wait_ge(out_written, past(stored * 16))
                normalized().then_inc(xn_ready, 1)
                v.drain()
            if whole:
                with v.Fori(0, whole) as c:
                    finish(c, c)
            stored = whole
            for c in range(whole, C):
                finish(c, stored)
                size = N - c * CH
                stored += (size >= P) + (size % P > 0)

        @block.vector
        def _(v):
            for t, x in ((chunk[96:97, :], 1.0), (nh[64:65, :], 1.0), (si[:, :], 0.0), (w23[:, :], 0.0), (lin2[:, :], 0.0), (ones[:, :], 1.0),
                         (zrow[:, :], 0.0), (w1[:, :], 0.0), (featT[:, :, :], 0.0), (rest3[:, :], 0.0), (first3[:, :, :], 0.0), (eps[:, :], EPS), (unit[:, :], 1.0), (zeros[:, :], 0.0), (hidT[64:65, :, :], 1.0)):
                v.memset(t, x)
            v.drain().then_inc(const_ready, 1)
            v.memset(xn[:, :, 32:33], 1.0)
            v.memset(xs[:, :, :], 0.0)
            v.drain().then_inc(const_ready, 1)
            v.wait_ge(const_in, 16 * len(CONSTS))
            v.tensor_scalar(w2[:, 64:128], w2[:, 64:128], 1.0 / math.sqrt(3.0), None, ALU.mult)
            v.scalar_tensor_tensor(fold0[64:96, :], si[64:96, :], 1.0 / math.sqrt(8.0), fold0[64:96, :], ALU.mult, ALU.add)
            v.tensor_tensor(lin2[64:96, :], lin2[64:96, :], fold1[64:96, :], ALU.add)
            v.wait_ge(weights_mm, 1)
            for k in range(2):
                v.tensor_scalar(mix[:, k, 0:8], bank(0)[:, 16 * k:16 * k + 8], wsel_c[:, k, 0:1], None, ALU.mult)
                for m in range(3):
                    v.tensor_scalar(mix[:, k, 8 + m:32:3], bank(0)[:, 16 * k + 8:16 * k + 16], wsel_c[:, k, 1 + m:2 + m],
                                    None, ALU.mult)
            v.tensor_scalar(nu[:, 0:32], bank(1)[:, 0:32], -1.0, None, ALU.mult)
            v.tensor_copy(nu[:, 32:33], bank(1)[:, 32:33])
            v.drain().then_inc(const_ready, 1)
            for k in range(GA):
                v.wait_ge(prep_in, 16 * (k + 2))
                view = span_in[0:GP, :] if GP <= W else junk[0:GP, :].bitcast(I32)
                v.tensor_reduce(gmin[0:GP, 0, k:k + 1], view, AX.X, ALU.min)
                v.tensor_reduce(gmin[0:GP, 1, k:k + 1], view, AX.X, ALU.max)
                v.drain().then_inc(prep_min, 1)
            v.tensor_tensor(gmin[0:GP, 2, :], gmin[0:GP, 1, :], gmin[0:GP, 0, :], ALU.subtract)
            v.drain().then_inc(prep_min, 1)
            v.wait_ge(prep_back, 32)
            v.tensor_reduce(stat[0:1, 0, 0:1], junk[0:1, 0:G], AX.X, ALU.max)
            v.tensor_copy(base_i[:, :], base_f[0:1, :])
            v.tensor_scalar(node_of[:, :], base_f[:, :], pcol[:, 0:1], None, ALU.add)
            v.drain()
            v.tensor_scalar(node_steep[:, :], node_of[0:W, :], STEEP, None, ALU.mult)
            v.tensor_scalar(narrow_i[:, :], stat[0:1, 0, 0:1], float(W) - 0.5, None, ALU.is_gt)
            v.drain().then_inc(flag_ready, 1)
            is_wide = v.value_load(narrow_i[0:1, 0:1], min_val=0, max_val=1)
            with v.If(is_wide == 0):
                v.tensor_tensor(rel[:, :].rearrange("p (g t) -> p g t", t=T), dst_all[:, :].rearrange("p (g t) -> p g t", t=T),
                                base_f[:, :].unsqueeze(2).to_broadcast([P, G, T]), ALU.subtract)
                v.drain().then_inc(rel_ready, 1)
                dve_program(v, False)
            with v.Else():
                v.tensor_copy(rel[:, :], dst_all[:, :])
                v.drain().then_inc(rel_ready, 1)
                dve_program(v, True)

def _cg_tables():
    import numpy as np
    f = math.factorial

    def coeff(j1, m1, j2, m2, j3, m3):
        if m3 != m1 + m2:
            return 0.0
        pref = (2 * j3 + 1) * f(j3 + j1 - j2) * f(j3 - j1 + j2) * f(j1 + j2 - j3) / f(j1 + j2 + j3 + 1)
        pref *= f(j3 + m3) * f(j3 - m3) * f(j1 - m1) * f(j1 + m1) * f(j2 - m2) * f(j2 + m2)
        s = 0.0
        for v in range(max(0, j2 - j3 - m1, j1 + m2 - j3), min(j1 + j2 - j3, j1 - m1, j2 + m2) + 1):
            s += (-1) ** v / (f(v) * f(j1 + j2 - j3 - v) * f(j1 - m1 - v) * f(j2 + m2 - v)
                              * f(j3 - j2 + m1 + v) * f(j3 - j1 - m2 + v))
        return math.sqrt(pref) * s

    def q(l):
        m_ = np.zeros((2 * l + 1, 2 * l + 1), np.complex128)
        for m in range(-l, 0):
            m_[l + m, l + abs(m)] = 1 / np.sqrt(2)
            m_[l + m, l - abs(m)] = -1j / np.sqrt(2)
        m_[l, l] = 1.0
        for m in range(1, l + 1):
            m_[l + m, l + abs(m)] = (-1) ** m / np.sqrt(2)
            m_[l + m, l - abs(m)] = 1j * (-1) ** m / np.sqrt(2)
        return (-1j) ** l * m_

    out = []
    for l1, l2, l3 in ((0, 0, 0), (0, 1, 1), (1, 0, 1), (1, 1, 0), (1, 1, 1), (2, 1, 1)):
        c = np.zeros((2 * l1 + 1, 2 * l2 + 1, 2 * l3 + 1), np.complex128)
        for m1 in range(-l1, l1 + 1):
            for m2 in range(-l2, l2 + 1):
                if -l3 <= m1 + m2 <= l3:
                    c[m1 + l1, m2 + l2, m1 + m2 + l3] = coeff(l1, m1, l2, m2, l3, m1 + m2)
        c = np.einsum("ij,kl,mn,ikn->jlm", q(l1), q(l2), np.conj(q(l3)).T, c).real
        out.append(c / np.linalg.norm(c))
    return out


def _constants():
    import numpy as np
    f32 = np.float32
    c = {"c_ident": np.eye(P, dtype=f32), "c_iota": np.tile(np.arange(W, dtype=f32), (P, 1))}
    c["c_tri"] = np.tril(np.ones((P, P), f32), -1)
    fold0 = np.zeros((96, 32), f32)
    fold0[0:32, :] = 0.25 * np.eye(32, dtype=f32)
    for m in range(3):
        for o in range(8):
            fold0[32 + m * 8 + o, 8 + o * 3 + m] = 0.25
    fold0[64:96] = np.eye(32)
    fold1 = np.zeros((96, 32), f32)
    fold1[0:32] = np.eye(32)
    fold1[64:96] = np.eye(32)
    c["c_fold0"], c["c_fold1"] = fold0, fold1
    cg = _cg_tables()
    pick = np.zeros((48, 4, P), f32)
    coef = np.zeros((P, 2, 4), f32)
    for chunk in range(2):
        for r in range(P if chunk == 0 else 120):
            if chunk == 0:
                k, f = divmod(r, 32)
            else:
                k, f = 4 + r // 24, 8 + r % 24
            scalar = f < 8
            ch, j = (f, 0) if scalar else divmod(f - 8, 3)
            i = 0 if k == 0 else k - 1 if k < 4 else k - 4
            zero = {True: 0, False: None}[scalar] if k == 0 else (3 if (k < 4 and not scalar) else None)
            one = (None if scalar else 1) if k == 0 else (2 if scalar else 4) if k < 4 else 5
            if zero is not None:
                pick[zero * 8 + ch, 2 * chunk, r] = 1
                coef[r, chunk, 0] = cg[zero][i, j, 0]
            if one is not None:
                pick[one * 8 + ch, 2 * chunk + 1, r] = 1
                coef[r, chunk, 1:4] = cg[one][i, j, :]
    c["c_wsel_r"], c["c_wsel_c"] = pick, coef
    return c


def kernel(**inputs):
    import numpy as np
    import concourse.bacc as _bacc
    from concourse.bass_utils import run_bass_kernel_spmd as _run

    given = {k: np.ascontiguousarray(v) for k, v in inputs.items()}
    n = given["x"].shape[0]
    e = given["src"].shape[0]
    g = e // E
    nt = -(-(n + W) // CH) * CH
    c = _constants()
    c["c_pcol"] = np.stack([np.arange(P) % W, nt + np.arange(P)], 1).astype(np.float32)
    arrays = dict(c)
    for k in ("x", "src", "dst", "edge_attr_4", "edge_attr_3", "edge_attr_5", "edge_weight1", "L0_gnn_W1", "L0_gnn_W2",
              "L0_gnn_si_w0", "L0_gnn_si_w1", "L1_gnn_W", "L2_gnn_w2_W", "L2_gnn_a", "L3_gnn_W1f", "L3_gnn_W1b",
              "L3_gnn_W2f", "L3_gnn_W2b", "L3_gnn_W1n", "L3_gnn_W2n"):
        arrays[k] = given[k]
    for k in ("L0_gnn_b1", "L3_gnn_b1f", "L3_gnn_b1b", "L3_gnn_b1n"):
        arrays[k] = given[k].reshape(-1, 1)
    for k in ("L0_gnn_b2", "L2_gnn_w1_b", "L2_gnn_w2_b", "L3_gnn_b2f", "L3_gnn_b2b", "L3_gnn_b2n"):
        arrays[k] = given[k].reshape(1, -1)
    def tiled(v):
        return v.reshape(g, P, T, -1).transpose(3, 0, 2, 1).reshape(-1, e)
    arrays["featT"] = np.ascontiguousarray(tiled(given["edge_attr_32"]))
    arrays["attrT"] = np.ascontiguousarray(tiled(given["edge_attr_16"]))
    arrays["dst_tp"] = np.ascontiguousarray(tiled(given["dst"]).reshape(-1))
    arrays["src_tp"] = np.ascontiguousarray(tiled(given["src"]).reshape(-1))
    arrays["dst_pg"] = np.ascontiguousarray(given["dst"].reshape(g, P, T).transpose(1, 0, 2).reshape(P, g * T))
    arrays["w1_WT"] = np.ascontiguousarray(given["L2_gnn_w1_W"].T)
    arrays["w2_WT"] = np.ascontiguousarray(given["L2_gnn_w2_W"].T)
    xt = np.zeros((32, nt), np.float32)
    xt[:, :n] = given["x"].T
    arrays["xT"] = xt

    nc = _bacc.Bacc("TRN2", target_bir_lowering=False, num_devices=1)
    a = {k: nc.dram_tensor(f"in_{k}", v.shape, mybir.dt.from_np(v.dtype), kind="ExternalInput").ap()
         for k, v in arrays.items()}
    out = nc.dram_tensor("out_x", [n, 32], F32, kind="ExternalOutput").ap()
    graph_kernel(nc, a, out)
    r = _run(nc, [{f"in_{k}": v for k, v in arrays.items()}], core_ids=[0])
    return r.results[0]["out_x"]
```
